# Optimizing a Trainium2 kernel written in Bass

```python
import numpy as np
import jax
import jax.numpy as jnp

def _softmax(x, axis=-1):
    return jax.nn.softmax(x, axis=axis)

def _gelu(x):
    return jax.nn.gelu(x, approximate=True)

def _silu(x):
    return jax.nn.silu(x)

def _sigmoid(x):
    return jax.nn.sigmoid(x)

def _layernorm(x, axis=-1, eps=1e-05):
    m = jnp.mean(x, axis=axis, keepdims=True)
    v = jnp.var(x, axis=axis, keepdims=True)
    return (x - m) / jnp.sqrt(v + eps)

def _scatter_add(tgt, idx, src, axis=0):
    return tgt.at[idx].add(src)

def _segment_sum(src, seg, n):
    return jax.ops.segment_sum(src, seg, n)
kernel_name = 'mk_gnn_resnorm_d1_gnn_r8_c44cd2'

def setup_inputs(seed: int=0):
    np.random.seed(seed)
    _w = jnp.asarray

    def _rec_inputs():
        import jax
        import jax.numpy as jnp
        _gk = jax.random.key(seed)
        x = -0.000202 + 1 * jax.random.normal(jax.random.fold_in(_gk, 1), (6250, 128), jnp.float32)
        src = jax.random.randint(jax.random.fold_in(_gk, 2), (100000,), 0, 6250, jnp.int32)
        dst = jax.random.randint(jax.random.fold_in(_gk, 3), (100000,), 0, 6250, jnp.int32)
        _o = jnp.argsort(dst, stable=True)
        src = src[_o]
        dst = dst[_o]
        return (x, src, dst)
    x, src, dst = _rec_inputs()

    def _L0_gnn_setup():
        import jax, jax.numpy as jnp
        import numpy as np
        N_NODES = 6250

        def _gnn_layer(x, W, b, src, dst):
            msg = x[src] @ W.T + b
            summed = jax.ops.segment_sum(msg, dst, num_segments=N_NODES)
            cnt = jax.ops.segment_sum(jnp.ones((src.shape[0],), msg.dtype), dst, num_segments=N_NODES)
            return summed / jnp.maximum(cnt, 1.0)[:, None]
        key = jax.random.key(seed)
        k1, k2, k3, k4, k5, k6 = jax.random.split(key, 6)
        in_c, hid_c, out_c = (128, 128, 128)
        E = 100000
        x = jax.random.normal(k1, (N_NODES, in_c), dtype=jnp.float32)
        edge_index = jax.random.randint(k2, (2, E), 0, N_NODES, dtype=jnp.int64)
        s1 = 1.0 / np.sqrt(in_c)
        s2 = 1.0 / np.sqrt(hid_c)
        W1 = jax.random.uniform(k3, (hid_c, in_c), jnp.float32, -s1, s1)
        b1 = jax.random.uniform(k4, (hid_c,), jnp.float32, -s1, s1)
        W2 = jax.random.uniform(k5, (out_c, hid_c), jnp.float32, -s2, s2)
        b2 = jax.random.uniform(k6, (out_c,), jnp.float32, -s2, s2)
        return {'x': x, 'edge_index': edge_index, 'W1': W1, 'b1': b1, 'W2': W2, 'b2': b2}
    _L0_gnn_all = _L0_gnn_setup()
    _L0_gnn_in = {k: v for k, v in _L0_gnn_all.items() if k in ('W1', 'b1', 'W2', 'b2')}
    del _L0_gnn_all
    return {'x': x, 'src': src, 'dst': dst, 'L0_gnn_W1': _L0_gnn_in['W1'], 'L0_gnn_b1': _L0_gnn_in['b1'], 'L0_gnn_W2': _L0_gnn_in['W2'], 'L0_gnn_b2': _L0_gnn_in['b2']}

def reference(x, src, dst, L0_gnn_W1, L0_gnn_b1, L0_gnn_W2, L0_gnn_b2):
    import jax
    import jax.numpy as jnp

    def _L0_gnn_ref(x, edge_index, W1, b1, W2, b2):
        import jax, jax.numpy as jnp
        import numpy as np
        N_NODES = 6250

        def _gnn_layer(x, W, b, src, dst):
            msg = x[src] @ W.T + b
            summed = jax.ops.segment_sum(msg, dst, num_segments=N_NODES)
            cnt = jax.ops.segment_sum(jnp.ones((src.shape[0],), msg.dtype), dst, num_segments=N_NODES)
            return summed / jnp.maximum(cnt, 1.0)[:, None]
        src, dst = (edge_index[0], edge_index[1])
        h = _gnn_layer(x, W1, b1, src, dst)
        h = jax.nn.relu(h)
        out = _gnn_layer(h, W2, b2, src, dst)
        return out
    edge_index = jnp.stack([src, dst])
    x = _layernorm(x + _L0_gnn_ref(x, edge_index, L0_gnn_W1, L0_gnn_b1, L0_gnn_W2, L0_gnn_b2), axis=-1)
    return x

_drawn_inputs = setup_inputs


def setup_inputs(seed=0):
    import zlib

    import numpy as np

    out = dict(_drawn_inputs(seed))
    spreads = {}
    factors = {'L0_gnn_W1': 4.237, 'L0_gnn_b1': 3.947}
    for name, (base, spread) in spreads.items():
        noise = np.random.default_rng([zlib.crc32(name.encode()), seed]).standard_normal(out[name].shape)
        drawn = base * np.exp(spread * noise) if base else spread * noise
        out[name] = jnp.asarray(drawn.astype(out[name].dtype))
    for name, factor in factors.items():
        out[name] = (out[name] * factor).astype(out[name].dtype)
    return out
```

```python
from contextlib import ExitStack

import numpy as np
import concourse.bass as bass
from concourse import mybir

P = 128
ALU = mybir.AluOpType
ACT = mybir.ActivationFunctionType
AX = mybir.AxisListType
F32 = mybir.dt.float32
BF16 = mybir.dt.bfloat16
I32 = mybir.dt.int32
I16 = mybir.dt.int16

EPS = 1e-5
TILES = 8
GROUP_EDGES = TILES * P
MARGIN = 40
SLOTS = 4
PARTS = 3


def split_of_tail(edges):
    for tiles in range(1, edges + 1):
        if edges % tiles == 0 and edges // tiles <= P:
            return tiles, edges // tiles


def gnn_resnorm(nc, x, src_groups, dst_groups, src_tail, dst_tail, w1t, b1, w2t, b2, out):
    N, C = x.shape
    NG = src_groups.shape[1]
    E = NG * GROUP_EDGES + src_tail.shape[0] * src_tail.shape[1]
    TT, TP = src_tail.shape[1], src_tail.shape[0]
    G = NG + 1
    NB = -(-N // P)
    LASTN = N - (NB - 1) * P
    SHARE = N * GROUP_EDGES // E
    W = SHARE + 2 * MARGIN
    OLD = W - SHARE
    ROW = PARTS * C
    BODIES = (NG - 1) // SLOTS
    AGGW = NB * P + 2 * MARGIN + SHARE
    CHUNK = 448
    NCHUNK = NB * P // CHUNK
    XCH = 7
    NXCH = NB // XCH
    assert C == P and SHARE * E == N * GROUP_EDGES and NCHUNK * CHUNK == NB * P and NXCH * XCH == NB
    assert NG == BODIES * SLOTS + 1 and 2 * SHARE == P and MARGIN <= SHARE

    with ExitStack() as ctx:
        def sb(name, shape, dt):
            return ctx.enter_context(nc.sbuf_tensor(name, shape, dt))

        def ps(name, shape, dt):
            return ctx.enter_context(nc.psum_tensor(name, shape, dt))

        def sem(name):
            return ctx.enter_context(nc.semaphore(name))

        xtab = nc.dram_tensor("xtab", (NB * P, ROW), BF16).ap()
        htab = nc.dram_tensor("htab", (NB * P, ROW), BF16).ap()
        tables = [xtab, htab]

        xf = sb("xf", [P, NB, C], F32)
        xs = sb("xs", [P, 2, XCH, ROW], BF16)
        xr = sb("xr", [P, 2, XCH, C], F32)
        idx_all = sb("idx_all", [P, G * TILES], I32)
        dst_all = sb("dst_all", [P, G * TILES], I32)
        base_all = sb("base_all", [P, G * TILES], I32)
        rel_all = sb("rel_all", [P, G * TILES], F32)
        agg = sb("agg", [P, AGGW], F32)
        cnt = sb("cnt", [P, AGGW], F32)
        nodes = sb("nodes", [P, NB * P], I16)
        msg = sb("msg", [P, SLOTS, TILES, ROW], BF16)
        onehot = sb("onehot", [P, SLOTS, TILES, W], BF16)
        wide_onehot = sb("wide_onehot", [P, TILES, CHUNK], BF16)
        idx = sb("idx", [P, SLOTS, TILES], I32)
        rel = sb("rel", [P, SLOTS, TILES], F32)
        ones = sb("ones", [P, P], BF16)
        onesf = sb("onesf", [P, P], F32)
        wt = sb("wt", [P, 2, C], F32)
        bias = sb("bias", [1, 2, C], F32)
        lim = sb("lim", [P, 4], F32)
        bad = sb("bad", [P, 1], F32)
        flag = sb("flag", [P, 1], I32)
        eps = sb("eps", [P, 1], F32)
        c1 = sb("c1", [P, C], F32)
        rc = sb("rc", [P, C], F32)
        mean = sb("mean", [P, C], F32)
        has = sb("has", [1, C], F32)
        h32 = sb("h32", [P, C], F32)
        hr = sb("hr", [P, C], F32)
        hs = sb("hs", [P, 2, ROW], BF16)
        y = sb("y", [P, C], F32)
        stats = sb("stats", [P, 6], F32)
        mv = sb("mv", [P, 2], F32)
        std = sb("std", [P, 1], F32)
        rstd = sb("rstd", [P, 1], F32)
        yo = sb("yo", [P, 2, C], F32)

        ps_sum = [ps(f"ps_sum{k}", [P, 512], F32) for k in range(2)]
        ps_cnt = [ps(f"ps_cnt{k}", [P, 512], F32) for k in range(2)]
        ps_lin = ps("ps_lin", [P, 512], F32)
        ps_bad = ps("ps_bad", [P, 512], F32)

        edges_in = sem("edges_in")
        tail_set = sem("tail_set")
        weights_in = sem("weights_in")
        x_in = [sem(f"x_in{c}") for c in range(NXCH)]
        iota_set = sem("iota_set")
        consts_set = sem("consts_set")
        pad_set = sem("pad_set")
        first_part = sem("first_part")
        rest_of_x = sem("rest_of_x")
        parts_done = sem("parts_done")
        xtab_out = [sem(f"xtab_out{k}") for k in range(2)]
        checked = sem("checked")
        bad_sum = sem("bad_sum")
        flag_set = sem("flag_set")

        onehot_ready = sem("onehot_ready")
        idx_ready = sem("idx_ready")
        rel_ready = sem("rel_ready")
        gathered = [sem(f"gathered{k}") for k in range(SLOTS)]
        summed = sem("summed")
        added = sem("added")
        mean_step = [sem(f"mean_step{l}") for l in range(2)]
        linear_done = [sem(f"linear_done{l}") for l in range(2)]
        relu_done = sem("relu_done")
        split_step = sem("split_step")
        norm_step = sem("norm_step")
        std_done = sem("std_done")
        stats_read = sem("stats_read")
        gather_begun = sem("gather_begun")
        h_out = [sem(f"h_out{k}") for k in range(2)]
        y_out = [sem(f"y_out{k}") for k in range(2)]
        cleared = sem("cleared")

        block = ctx.enter_context(nc.Block())

        def full_rounds(slot):
            return len(range(slot, NG, SLOTS))

        TAIL_SLOT = NG % SLOTS

        def gathers_before(layer, slot):
            return layer * 16 * (full_rounds(slot) * TILES + (TT if slot == TAIL_SLOT else 0))

        def gathered_by(layer, g, slot, rnd):
            if isinstance(g, int) and g == NG:
                return gathers_before(layer + 1, slot)
            return (rnd + 1) * (16 * TILES) + gathers_before(layer, slot)

        def tiles_of(g):
            return (TT, TP) if isinstance(g, int) and g == NG else (TILES, P)

        def split_x_first(act):
            for c in range(NXCH):
                act.wait_ge(x_in[c], 32 if c == NXCH - 1 else 16)
                if c >= 2:
                    act.wait_ge(xtab_out[c % 2], 16 * (c // 2))
                nc.scalar.activation(xs[:, c % 2, :, 0:C], xf[:, c * XCH:(c + 1) * XCH, :],
                                     ACT.Copy).then_inc(first_part, 1)
                act.wait_ge(rest_of_x, c + 1)
                nc.scalar.activation(xs[:, c % 2, :, C:2 * C], xr[:, c % 2, :, :],
                                     ACT.Copy).then_inc(first_part, 1)

        def split_x_rest(dve, c):
            dve.wait_ge(first_part, 2 * c + 1)
            nc.vector.tensor_tensor(xr[:, c % 2, :, :], xf[:, c * XCH:(c + 1) * XCH, :],
                                    xs[:, c % 2, :, 0:C], ALU.subtract).then_inc(rest_of_x, 1)
            dve.wait_ge(rest_of_x, c + 1)
            dve.wait_ge(first_part, 2 * c + 2)
            nc.vector.tensor_tensor(xs[:, c % 2, :, 2 * C:3 * C], xr[:, c % 2, :, :],
                                    xs[:, c % 2, :, C:2 * C], ALU.subtract).then_inc(parts_done, 1)

        @block.sync
        def _(sp):
            sp.wait_ge(tail_set, 2)
            sp.dma_start(dst_all[:, 0:NG * TILES], dst_groups.rearrange("p g j -> p (g j)")).then_inc(edges_in, 16)
            sp.dma_start(dst_all[0:TP, NG * TILES:NG * TILES + TT], dst_tail).then_inc(edges_in, 16)
            sp.dma_start(idx_all[:, 0:NG * TILES], src_groups.rearrange("p g j -> p (g j)")).then_inc(edges_in, 16)
            sp.dma_start(idx_all[0:TP, NG * TILES:NG * TILES + TT], src_tail).then_inc(edges_in, 16)
            for c in range(NXCH):
                lo, hi = c * XCH, (c + 1) * XCH
                if hi < NB:
                    sp.dma_start(xf[:, lo:hi, :], x[lo * P:hi * P, :].rearrange("(b p) c -> p b c", p=P)
                                 ).then_inc(x_in[c], 16)
                else:
                    sp.wait_ge(pad_set, 1)
                    sp.dma_start(xf[:, lo:hi - 1, :], x[lo * P:(hi - 1) * P, :].rearrange("(b p) c -> p b c", p=P)
                                 ).then_inc(x_in[c], 16)
                    sp.dma_start(xf[0:LASTN, NB - 1, :], x[(NB - 1) * P:N, :]).then_inc(x_in[c], 16)
            sp.dma_start(wt[:, 0, :], w1t).then_inc(weights_in, 16)
            sp.dma_start(wt[:, 1, :], w2t).then_inc(weights_in, 16)
            sp.dma_start(bias[:, 0, :], b1).then_inc(weights_in, 16)
            sp.dma_start(bias[:, 1, :], b2).then_inc(weights_in, 16)
            for c in range(NXCH):
                sp.wait_ge(parts_done, c + 1)
                sp.dma_start(xtab[c * XCH * P:(c + 1) * XCH * P, :].rearrange("(b p) c -> p b c", p=P),
                             xs[:, c % 2, :, :]).then_inc(xtab_out[c % 2], 16)

            def store_h(b, parity):
                sp.wait_ge(split_step, b * 3 + 3)
                sp.dma_start(htab[bass.ds(b * P, P), :], hs[:, parity, :]).then_inc(h_out[parity], 16)

            def store_y(b, parity):
                sp.wait_ge(norm_step, b * 5 + 5)
                rows = LASTN if isinstance(b, int) and b == NB - 1 else P
                sp.dma_start(out[bass.ds(b * P, rows), :], yo[0:rows, parity, :]).then_inc(y_out[parity], 16)

            for store in (store_h, store_y):
                with sp.Fori(0, NB // 2) as i:
                    store(i * 2, 0)
                    store(i * 2 + 1, 1)
                store(NB - 1, 0)
            for k in range(2):
                sp.wait_ge(h_out[k], 16 * len(range(k, NB, 2)))
                sp.wait_ge(y_out[k], 16 * len(range(k, NB, 2)))

        @block.gpsimd
        def _(pool):
            nc.gpsimd.memset(idx_all[:, NG * TILES:], 0).then_inc(tail_set, 1)
            nc.gpsimd.memset(dst_all[:, NG * TILES:], N - 1).then_inc(tail_set, 1)
            nc.gpsimd.memset(xf[:, NB - 1, :], 0.0).then_inc(pad_set, 1)
            nc.gpsimd.memset(eps[:], EPS).then_inc(consts_set, 1)
            nc.gpsimd.iota(base_all[:].rearrange("p (g j) -> p g j", j=TILES), [[SHARE, G], [0, TILES]],
                           base=-MARGIN, channel_multiplier=0).then_inc(iota_set, 1)
            nc.gpsimd.iota(nodes[:], [[1, NB * P]], base=0, channel_multiplier=0).then_inc(iota_set, 1)
            nc.gpsimd.memset(onesf[:], 1.0).then_inc(consts_set, 1)
            nc.gpsimd.memset(ones[:], 1.0).then_inc(consts_set, 1)

            def table_ready(layer):
                if layer == 0:
                    for k in range(2):
                        pool.wait_ge(xtab_out[k], 16 * len(range(k, NXCH, 2)))
                else:
                    for k in range(2):
                        pool.wait_ge(h_out[k], 16 * len(range(k, NB, 2)))

            def gather(layer, g, slot, groups_done):
                tiles, parts = tiles_of(g)
                table_ready(layer)
                pool.wait_ge(idx_ready, groups_done + 1)
                pool.sem_inc(gather_begun, 1)
                for j in range(tiles):
                    nc.gpsimd.indirect_dma_start(
                        out=msg[0:parts, slot, j, :], out_offset=None, in_=tables[layer],
                        in_offset=bass.IndirectOffsetOnAxis(ap=idx[0:parts, slot, j:j + 1], axis=0),
                    ).then_inc(gathered[slot], 16)

            def fast():
                for layer in range(2):
                    with pool.Fori(0, BODIES) as i:
                        for k in range(SLOTS):
                            gather(layer, i * SLOTS + k, k, i * SLOTS + k + layer * G)
                    for g in range(BODIES * SLOTS, G):
                        gather(layer, g, g % SLOTS, g + layer * G)

            def general():
                for layer in range(2):
                    with pool.Fori(0, NG) as g:
                        gather(layer, g, 0, g + layer * G)
                    gather(layer, NG, 0, NG + layer * G)

            pool.wait_ge(flag_set, 1)
            violated = pool.value_load(flag[0:1, 0:1], min_val=0, max_val=P)
            with pool.If(violated):
                general()
            with pool.Else():
                fast()

        @block.tensor
        def _(pe):
            pe.wait_ge(consts_set, 3)
            pe.wait_ge(checked, 6)
            pe.matmul(ps_bad[:, 0:1], onesf[:], bad[:], start=True, stop=True).then_inc(bad_sum, 1)
            pe.wait_ge(weights_in, 64)

            def sum_rows(sums, counts, rows, hot, tiles, parts):
                for j in range(tiles):
                    for s in range(PARTS):
                        mm = pe.matmul(sums, rows[0:parts, j, s * C:(s + 1) * C], hot[0:parts, j, :],
                                       start=(j == 0 and s == 0), stop=(j == tiles - 1 and s == PARTS - 1))
                if counts is not None:
                    for j in range(tiles):
                        mm = pe.matmul(counts, ones[0:parts, :], hot[0:parts, j, :],
                                       start=(j == 0), stop=(j == tiles - 1))
                mm.then_inc(summed, 1)

            def linear(layer, b):
                pe.wait_ge(mean_step[layer], b * 4 + 4)
                if layer == 0:
                    pe.wait_ge(relu_done, b * 2)
                else:
                    pe.wait_ge(norm_step, b * 5)
                pe.matmul(ps_lin[:, 0:C], mean[:], wt[:, layer, :], start=True, stop=False)
                pe.matmul(ps_lin[:, 0:C], has[:], bias[:, layer, :], start=False, stop=True
                          ).then_inc(linear_done[layer], 1)

            def fast():
                for layer in range(2):
                    def group(g, slot, rnd, first=False):
                        tiles, parts = tiles_of(g)
                        n = g + layer * G
                        pe.wait_ge(onehot_ready, n + 1)
                        pe.wait_ge(gathered[slot], gathered_by(layer, g, slot, rnd))
                        if not first:
                            pe.wait_ge(added, n - 1)
                        sum_rows(ps_sum[slot % 2][:, 0:W], ps_cnt[slot % 2][:, 0:W] if layer == 0 else None,
                                 msg[:, slot], onehot[:, slot], tiles, parts)
                    for k in range(SLOTS):
                        group(k, k, 0, first=(layer == 0 and k < 2))
                    if layer == 1:
                        pe.wait_ge(relu_done, 2 * NB)
                    with pe.Fori(1, BODIES) as i:
                        for k in range(SLOTS):
                            group(i * SLOTS + k, k, i)
                            if k % 2 == 0:
                                linear(layer, i * 2 - 2 + k // 2)
                    group(NG - 1, 0, BODIES)
                    linear(layer, NB - 3)
                    group(NG, 1, BODIES)
                    linear(layer, NB - 2)
                    linear(layer, NB - 1)

            def general():
                for layer in range(2):
                    def chunk(n, c, tiles, parts, landed):
                        q = n * NCHUNK + c
                        pe.wait_ge(gathered[0], landed)
                        pe.wait_ge(onehot_ready, q + 1)
                        pe.wait_ge(added, q)
                        sum_rows(ps_sum[0][:, 0:CHUNK], ps_cnt[0][:, 0:CHUNK], msg[:, 0], wide_onehot[:],
                                 tiles, parts)
                    with pe.Fori(0, NG) as g:
                        landed = (g + 1) * (16 * TILES) + layer * 16 * (NG * TILES + TT)
                        with pe.Fori(0, NCHUNK) as c:
                            chunk(g + layer * G, c, TILES, P, landed)
                    with pe.Fori(0, NCHUNK) as c:
                        chunk(NG + layer * G, c, TT, TP, (layer + 1) * 16 * (NG * TILES + TT))
                    if layer == 1:
                        pe.wait_ge(relu_done, 2 * NB)
                    with pe.Fori(0, NB) as b:
                        linear(layer, b)

            pe.wait_ge(flag_set, 1)
            violated = pe.value_load(flag[0:1, 0:1], min_val=0, max_val=P)
            with pe.If(violated):
                general()
            with pe.Else():
                fast()

        @block.scalar
        def _(act):
            split_x_first(act)

            def relu(b, parity):
                act.wait_ge(linear_done[0], b + 1)
                act.wait_ge(split_step, b * 3)
                act.wait_ge(h_out[parity], (b - parity) * 8)
                nc.scalar.activation(h32[:], ps_lin[:, 0:C], ACT.Relu).then_inc(relu_done, 1)
                nc.scalar.activation(hs[:, parity, 0:C], ps_lin[:, 0:C], ACT.Relu).then_inc(relu_done, 1)

            def deviation(b):
                act.wait_ge(norm_step, b * 5 + 3)
                nc.scalar.activation(std[:], mv[:, 1:2], ACT.Sqrt, bias=eps[:, 0:1]).then_inc(std_done, 1)

            with act.Fori(0, NB // 2) as i:
                relu(i * 2, 0)
                relu(i * 2 + 1, 1)
            relu(NB - 1, 0)
            with act.Fori(0, NB) as b:
                deviation(b)

        @block.vector
        def _(dve):
            dve.wait_ge(edges_in, 64)
            dve.wait_ge(iota_set, 2)
            nc.vector.tensor_tensor(rel_all[:], dst_all[:], base_all[:], ALU.subtract).then_inc(checked, 1)
            dve.wait_ge(checked, 1)
            nc.vector.tensor_reduce(lim[:, 0:1], rel_all[:], AX.X, ALU.min).then_inc(checked, 1)
            nc.vector.tensor_reduce(lim[:, 1:2], rel_all[:], AX.X, ALU.max).then_inc(checked, 1)
            dve.wait_ge(checked, 3)
            nc.vector.tensor_scalar(lim[:, 2:3], lim[:, 0:1], -0.5, None, ALU.is_lt).then_inc(checked, 1)
            nc.vector.tensor_scalar(lim[:, 3:4], lim[:, 1:2], W - 0.5, None, ALU.is_gt).then_inc(checked, 1)
            dve.wait_ge(checked, 5)
            nc.vector.tensor_tensor(bad[:], lim[:, 2:3], lim[:, 3:4], ALU.max).then_inc(checked, 1)
            dve.wait_ge(bad_sum, 1)
            nc.vector.tensor_copy(flag[:], ps_bad[:, 0:1]).then_inc(flag_set, 1)
            for c in range(NXCH):
                split_x_rest(dve, c)

            def to_mean(layer, b):
                col = b * P + MARGIN
                n = b * 4
                dve.wait_ge(linear_done[layer], b)
                nc.vector.tensor_scalar(c1[:], cnt[:, bass.ds(col, P)], 1.0, None, ALU.max
                                        ).then_inc(mean_step[layer], 1)
                nc.vector.tensor_scalar(has[:], cnt[0:1, bass.ds(col, P)], 1.0, None, ALU.min
                                        ).then_inc(mean_step[layer], 1)
                dve.wait_ge(mean_step[layer], n + 2)
                nc.vector.reciprocal(rc[:], c1[:]).then_inc(mean_step[layer], 1)
                dve.wait_ge(mean_step[layer], n + 3)
                nc.vector.tensor_tensor(mean[:], agg[:, bass.ds(col, P)], rc[:], ALU.mult
                                        ).then_inc(mean_step[layer], 1)

            def split_h(b, parity):
                n = b * 3
                dve.wait_ge(relu_done, b * 2 + 2)
                nc.vector.tensor_tensor(hr[:], h32[:], hs[:, parity, 0:C], ALU.subtract).then_inc(split_step, 1)
                dve.wait_ge(split_step, n + 1)
                nc.vector.tensor_copy(hs[:, parity, C:2 * C], hr[:]).then_inc(split_step, 1)
                dve.wait_ge(split_step, n + 2)
                nc.vector.tensor_tensor(hs[:, parity, 2 * C:3 * C], hr[:], hs[:, parity, C:2 * C],
                                        ALU.subtract).then_inc(split_step, 1)

            def norm(b, parity):
                n = b * 5
                dve.wait_ge(linear_done[1], b + 1)
                dve.wait_ge(norm_step, n)
                nc.vector.tensor_tensor(y[:].rearrange("p (o c) -> p o c", o=1),
                                        ps_lin[:, 0:C].rearrange("p (o c) -> p o c", o=1),
                                        xf[:, bass.ds(b, 1), :], ALU.add).then_inc(norm_step, 1)
                dve.wait_ge(norm_step, n + 1)
                nc.vector.bn_stats(stats[:], y[:]).then_inc(norm_step, 1)
                dve.wait_ge(norm_step, n + 2)
                dve.sem_inc(stats_read, 1)
                nc.vector.bn_aggr(mv[:], stats[:]).then_inc(norm_step, 1)
                dve.wait_ge(std_done, b + 1)
                nc.vector.reciprocal(rstd[:], std[:]).then_inc(norm_step, 1)
                dve.wait_ge(norm_step, n + 4)
                dve.wait_ge(y_out[parity], (b - parity) * 8)
                nc.vector.tensor_scalar(yo[:, parity, :], y[:], mv[:, 0:1], rstd[:, 0:1],
                                        ALU.subtract, ALU.mult).then_inc(norm_step, 1)

            def finish(layer, b, parity):
                if layer == 0:
                    split_h(b, parity)
                else:
                    norm(b, parity)

            def load_slot(g, slot, scalars):
                nc.vector.tensor_copy(idx[:, slot, :], idx_all[:, bass.ds(g * TILES, TILES)]).then_inc(idx_ready, 1)
                nc.vector.tensor_copy(rel[:, slot, :], scalars[:, bass.ds(g * TILES, TILES)]).then_inc(rel_ready, 1)

            def fast():
                for layer in range(2):
                    off = layer * G

                    def prepare(g, slot):
                        n = g + off
                        if not (isinstance(n, int) and n < SLOTS):
                            dve.wait_ge(summed, n - SLOTS + 1)
                        load_slot(g, slot, rel_all)
                        dve.wait_ge(rel_ready, n + 1)
                        for j in range(TILES):
                            op = nc.vector.tensor_scalar(onehot[:, slot, j, :], nodes[:, 0:W], rel[:, slot, j:j + 1],
                                                         None, ALU.is_equal)
                        op.then_inc(onehot_ready, 1)

                    def evacuate(g, slot):
                        n = g + off
                        dve.wait_ge(summed, n + 1)
                        dve.wait_ge(added, n)
                        old, new = bass.ds(g * SHARE, OLD), bass.ds(g * SHARE + OLD, SHARE)
                        if layer == 0:
                            nc.vector.tensor_tensor(cnt[:, old], cnt[:, old], ps_cnt[slot % 2][:, 0:OLD], ALU.add)
                            nc.vector.tensor_copy(cnt[:, new], ps_cnt[slot % 2][:, OLD:W])
                        nc.vector.tensor_tensor(agg[:, old], agg[:, old], ps_sum[slot % 2][:, 0:OLD], ALU.add)
                        nc.vector.tensor_copy(agg[:, new], ps_sum[slot % 2][:, OLD:W]).then_inc(added, 1)

                    if layer == 0:
                        nc.vector.memset(cnt[:, 0:OLD], 0.0).then_inc(cleared, 1)
                    nc.vector.memset(agg[:, 0:OLD], 0.0).then_inc(cleared, 1)
                    dve.wait_ge(cleared, 2 + layer)
                    prepare(0, 0)
                    for k in range(1, SLOTS):
                        prepare(k, k)
                        evacuate(k - 1, k - 1)
                    with dve.Fori(1, BODIES) as i:
                        for k in range(SLOTS):
                            prepare(i * SLOTS + k, k)
                            evacuate(i * SLOTS + (k - 1), (k - 1) % SLOTS)
                            if k % 2 == 0:
                                dve.wait_ge(added, i * SLOTS + (k + off))
                                to_mean(layer, i * 2 - 2 + k // 2)
                            else:
                                finish(layer, i * 2 - 2 + k // 2, k // 2)
                    prepare(NG - 1, 0)
                    evacuate(NG - 2, SLOTS - 1)
                    dve.wait_ge(added, NG - 1 + off)
                    to_mean(layer, NB - 3)
                    prepare(NG, 1)
                    evacuate(NG - 1, 0)
                    finish(layer, NB - 3, 0)
                    dve.wait_ge(added, NG + off)
                    to_mean(layer, NB - 2)
                    finish(layer, NB - 2, 1)
                    evacuate(NG, 1)
                    dve.wait_ge(added, G + off)
                    to_mean(layer, NB - 1)
                    finish(layer, NB - 1, 0)

            def general():
                for layer in range(2):
                    def all_chunks(g, n):
                        load_slot(g, 0, dst_all)
                        with dve.Fori(0, NCHUNK) as c:
                            q = n * NCHUNK + c
                            dve.wait_ge(rel_ready, n + 1)
                            for j in range(TILES):
                                op = nc.vector.tensor_scalar(wide_onehot[:, j, :], nodes[:, bass.ds(c * CHUNK, CHUNK)],
                                                             rel[:, 0, j:j + 1], None, ALU.is_equal)
                            op.then_inc(onehot_ready, 1)
                            dve.wait_ge(summed, q + 1)
                            at = bass.ds(c * CHUNK + MARGIN, CHUNK)
                            if layer == 0:
                                nc.vector.tensor_tensor(cnt[:, at], cnt[:, at], ps_cnt[0][:, 0:CHUNK], ALU.add)
                            nc.vector.tensor_tensor(agg[:, at], agg[:, at], ps_sum[0][:, 0:CHUNK], ALU.add
                                                    ).then_inc(added, 1)
                            dve.wait_ge(added, q + 1)

                    if layer == 0:
                        nc.vector.memset(cnt[:], 0.0).then_inc(cleared, 1)
                    nc.vector.memset(agg[:], 0.0).then_inc(cleared, 1)
                    dve.wait_ge(cleared, 2 + layer)
                    with dve.Fori(0, NG) as g:
                        all_chunks(g, g + layer * G)
                    all_chunks(NG, NG + layer * G)
                    with dve.Fori(0, NB // 2) as i:
                        for k in range(2):
                            to_mean(layer, i * 2 + k)
                            finish(layer, i * 2 + k, k)
                    to_mean(layer, NB - 1)
                    finish(layer, NB - 1, 0)

            dve.wait_ge(flag_set, 1)
            violated = dve.value_load(flag[0:1, 0:1], min_val=0, max_val=P)
            with dve.If(violated):
                general()
            with dve.Else():
                fast()


def kernel(x, src, dst, L0_gnn_W1, L0_gnn_b1, L0_gnn_W2, L0_gnn_b2):
    import numpy as _np
    import concourse.bacc as _bacc
    from concourse import mybir as _mybir
    from concourse.bass_utils import run_bass_kernel_spmd as _run

    src, dst = _np.asarray(src), _np.asarray(dst)
    full = src.shape[0] // GROUP_EDGES
    tiles, parts = split_of_tail(src.shape[0] - full * GROUP_EDGES)

    def groups(e):
        return _np.ascontiguousarray(e[:full * GROUP_EDGES].reshape(full, P, TILES).transpose(1, 0, 2))

    def tail(e):
        return _np.ascontiguousarray(e[full * GROUP_EDGES:].reshape(parts, tiles))

    arrays = {
        "x": _np.ascontiguousarray(x),
        "src_groups": groups(src), "dst_groups": groups(dst),
        "src_tail": tail(src), "dst_tail": tail(dst),
        "w1t": _np.ascontiguousarray(_np.asarray(L0_gnn_W1).T), "b1": _np.asarray(L0_gnn_b1).reshape(1, -1),
        "w2t": _np.ascontiguousarray(_np.asarray(L0_gnn_W2).T), "b2": _np.asarray(L0_gnn_b2).reshape(1, -1),
    }
    nc = _bacc.Bacc("TRN2", target_bir_lowering=False, num_devices=1)
    args = [nc.dram_tensor(n, a.shape, _mybir.dt.from_np(a.dtype), kind="ExternalInput").ap()
            for n, a in arrays.items()]
    args.append(nc.dram_tensor("out", x.shape, _mybir.dt.from_np(arrays["x"].dtype), kind="ExternalOutput").ap())
    gnn_resnorm(nc, *args)
    return _run(nc, [arrays], core_ids=[0]).results[0]["out"]
```

```python
from contextlib import ExitStack

import concourse.bass as bass
from concourse import mybir

P = 128
ALU = mybir.AluOpType
ACT = mybir.ActivationFunctionType
AX = mybir.AxisListType
F32 = mybir.dt.float32
BF16 = mybir.dt.bfloat16
I32 = mybir.dt.int32
I16 = mybir.dt.int16

EPS = 1e-5
TILES = 8
GROUP_EDGES = TILES * P
MARGIN = 40
SLOTS = 5
PARTS = 3
STEPS = 10
COUNTED = (14, 19)
CTILES = 18
PASS_BLOCKS = 7
SPAN = 36
HOT_TILES = 6
HOT_BUFS = 7
EXACT = 256
SORTED_COLS = 320
BUFS = 3
KEYS_AT = 5
LEAD = 3


def split_of_tail(edges):
    for tiles in range(1, edges + 1):
        if edges % tiles == 0 and edges // tiles <= P:
            return tiles, edges // tiles


def wait(eng, sem, value):
    if not (isinstance(value, int) and value <= 0):
        eng.wait_ge(sem, value)


def tile_first(t, share):
    return min(max(t * share + share // 2 - SPAN // 2, 0), P - SPAN)


def gnn_resnorm(nc, x, edge_list, src_groups, dst_groups, src_tail, dst_tail, w1t, b1, w2t, b2,
                windows, identity, out):
    N, C = x.shape
    NG = src_groups.shape[1]
    E = edge_list.shape[1]
    TT, TP = src_tail.shape[1], src_tail.shape[0]
    G = NG + 1
    NB = -(-N // P)
    LASTN = N - (NB - 1) * P
    SHARE = N * GROUP_EDGES // E
    W = SHARE + 2 * MARGIN
    OLD = W - SHARE
    ROW = PARTS * C
    AGGW = NB * P + 2 * MARGIN + SHARE
    CHUNK = 448
    NCHUNK = NB * P // CHUNK
    XCH = 8
    NXCH = NB // XCH + 1
    ROUNDS = (COUNTED[0] // 2, COUNTED[1] - COUNTED[0] + 1)
    FIRST = tuple(2 * k - 1 for k in COUNTED)
    LEFT = tuple(G - f - STEPS * r for f, r in zip(FIRST, ROUNDS))
    BEYOND = LEAD - 1
    GROUPS = tuple(G - f for f in FIRST)
    NPASS = NB // PASS_BLOCKS
    PASSW = PASS_BLOCKS * P
    HALVES = ((0, 4), (4, PASS_BLOCKS - 4))
    HOTW = PASS_BLOCKS * SPAN
    KEYCOLS = COUNTED[1] * CTILES
    TURN = P // CTILES
    NTURN = -(-COUNTED[1] // TURN)
    CHUNKS = CTILES // HOT_TILES
    NHOT = NPASS * CHUNKS
    assert C == P and SHARE * E == N * GROUP_EDGES and NCHUNK * CHUNK == NB * P and (NB - 1) % XCH == 0
    assert 2 * SHARE == P and MARGIN <= SHARE and NPASS * PASS_BLOCKS == NB
    EDGEW = (G + LEAD - LEFT[1]) * TILES
    assert LEFT == (1, 1) and 2 * ROUNDS[0] == COUNTED[0] and COUNTED[0] - 1 == 3 + 2 * (ROUNDS[1] - 1)
    assert HOT_BUFS >= 2 * CHUNKS and KEYCOLS <= 512 and STEPS % SLOTS == 0 and STEPS % 2 == 0 and NHOT % HOT_BUFS == 0
    assert SORTED_COLS * P >= ((COUNTED[1] * P + MARGIN) // SHARE + 1) * GROUP_EDGES

    OUTPUTS = ((0, 1, 2, 4, 5, 6, 8), (0, 1, 2, 3, 4, 6, 7, 8))
    OUTPUTS_FIRST = ((4, 5, 6, 8), (3, 4, 5, 6, 7, 8))
    OUTPUTS_LEFT = ((0, 1, 2), (0, 1, 2))

    def buffers(layer):
        count = len(OUTPUTS[layer])
        later = [1 if j == count - 1 and j % BUFS == 0 else j % BUFS for j in range(count)]
        return later[count - len(OUTPUTS_FIRST[layer]):], later, later[:len(OUTPUTS_LEFT[layer])]

    def output(layer, i, step):
        first, later, left = buffers(layer)
        if isinstance(i, int) and i == 0:
            j = OUTPUTS_FIRST[layer].index(step)
            buf = first[j]
            number, uses = j, first[:j].count(buf)
        else:
            last = isinstance(i, int) and i == ROUNDS[layer]
            j = (OUTPUTS_LEFT if last else OUTPUTS)[layer].index(step)
            buf = later[j]
            number = (i - 1) * len(later) + (len(first) + j)
            uses = (i - 1) * later.count(buf) + (first.count(buf) + later[:j].count(buf))
        if step % 2 == 0:
            block = i * (STEPS // 2) + (COUNTED[layer] - 2 + step // 2)
        elif layer == 0:
            block = i * 2 + (-1 if step == 1 else 0)
        elif step == 1:
            block = i + (COUNTED[0] - 2)
        elif isinstance(i, int) and i == 0:
            block = (step - 3) // 2
        else:
            block = i * 2 + (1 if step == 3 else 2)
        return number, block, buf, uses

    def buffer_uses(layer, buf):
        per = [order.count(buf) for order in buffers(layer)]
        return per[0] + per[1] * (ROUNDS[layer] - 1) + per[2]

    PASSES = (((0,), (1, 2), (3, 4), (5, 6), ()) * 2, ((0,), (1,), (2,), (3,), (4,), (5,), (6,), (), (), ()))

    APPLIED = (((), (0,), (1, 2), (3, 4), (5, 6)) * 2, ((),) * STEPS)

    def counted(layer, i, step):
        return i * 2 + step // 5 if layer == 0 else i + (COUNTED[0] - 1)

    def counts_at(layer, i):
        return not (layer == 1 and isinstance(i, int) and i == 0)

    with ExitStack() as ctx:
        def sb(name, shape, dt):
            return ctx.enter_context(nc.sbuf_tensor(name, shape, dt))

        def ps(name, shape, dt):
            return ctx.enter_context(nc.psum_tensor(name, shape, dt))

        def sem(name):
            return ctx.enter_context(nc.semaphore(name))

        xtab = nc.dram_tensor("xtab", (NB * P, ROW), BF16).ap()
        htab = nc.dram_tensor("htab", (NB * P, ROW), BF16).ap()
        ctab = nc.dram_tensor("ctab", (COUNTED[0] * P, NB * P), BF16).ap()
        tables = [xtab, htab]

        table = sb("table", [P, NB, ROW], BF16)
        edges_all = sb("edges_all", [P, 2, EDGEW], I32)
        idx_all = edges_all[:, 0, :]
        dst_all = sb("dst_all", [P, EDGEW], I32)
        base_all = edges_all[:, 1, :]
        rel_all = base_all.bitcast(F32)
        acc = sb("acc", [P, 2, AGGW], F32)
        agg = acc[:, 0, :]
        cnt = acc[:, 1, :]
        nodes = sb("nodes", [P, NB * SPAN], I16)
        msg = sb("msg", [P, SLOTS, TILES, ROW], BF16)
        onehot = sb("onehot", [P, SLOTS, TILES, W], BF16)
        edges = sb("edges", [P, SLOTS, 2, TILES], I32)
        idx = edges[:, :, 0, :]
        rel = edges[:].bitcast(F32)[:, :, 1, :]
        built = sb("built", [P, NB * P], BF16)
        loaded = sb("loaded", [P, NB * P], BF16)
        wide_onehot = built[:, 0:TILES * CHUNK].rearrange("p (j n) -> p j n", j=TILES)
        keys_all = sb("keys_all", [P, 2, KEYCOLS + CTILES], F32)
        keys = sb("keys", [P, 2, CTILES], F32)
        rowhot = sb("rowhot", [P, CTILES, P], BF16)
        colhot = sb("colhot", [P, HOT_BUFS, HOT_TILES, HOTW], BF16)
        xin = colhot[:].rearrange("p k t n -> p (k t n)").bitcast(F32)[:, 0:2 * XCH * C].rearrange(
            "p (k b c) -> p k b c", k=2, b=XCH)
        xrest = loaded[:].bitcast(F32)[:, 0:2 * XCH * C].rearrange("p (k b c) -> p k b c", k=2, b=XCH)
        scratch = msg[:].rearrange("p k t n -> p (k t n)").bitcast(F32)
        used = [0]

        def at_start(*shape):
            size = 1
            for n in shape:
                size *= n
            place = scratch[:, used[0]:used[0] + size]
            used[0] += size
            assert used[0] <= SLOTS * TILES * ROW // 2
            if len(shape) == 1:
                return place
            names = "abc"[:len(shape)]
            return place.rearrange(f"p ({' '.join(names)}) -> p {' '.join(names)}", **dict(zip(names, shape)))
        run0, run1, run256 = [at_start(SORTED_COLS).bitcast(I32) for k in range(3)]
        order = at_start(SORTED_COLS)
        win = at_start(2, KEYCOLS)
        lined = at_start(2, NTURN, P).bitcast(I32)
        lined_f32 = at_start(2, NTURN, P)
        before = scratch[:, used[0]:used[0] + COUNTED[1] * SORTED_COLS // 2].bitcast(BF16).rearrange(
            "p (b j) -> p b j", b=COUNTED[1])
        source, low = [at_start(KEYCOLS).bitcast(I32) for k in range(2)]
        from_block, from_window, not_before, inside, in_block, outside, column, column1 = [
            at_start(KEYCOLS) for k in range(8)]
        ones = sb("ones", [P, P], BF16)
        onesf = sb("onesf", [P, P], F32)
        zeros = sb("zeros", [1, 512], BF16)
        unit = sb("unit", [P, P], F32)
        wt = sb("wt", [P, 2, C], F32)
        bias = sb("bias", [1, 2, C], F32)
        lim = sb("lim", [P, 9], F32)
        tests = sb("tests", [P, 1 + COUNTED[1]], F32)
        sums = sb("sums", [P, 1 + COUNTED[1]], F32)
        span = sb("span", [P, COUNTED[1]], F32)
        starts = sb("starts", [P, 1 + COUNTED[1]], I32)
        flag = sb("flag", [P, 1], I32)
        eps = sb("eps", [P, 1], F32)
        taken = sb("taken", [P, 2, C], F32)
        degree = sb("degree", [P, 1], F32)
        rc = sb("rc", [P, 2], F32)
        h32 = sb("h32", [P, C], F32)
        hr = sb("hr", [P, C], F32)
        hs = sb("hs", [P, BUFS, ROW], BF16)
        xres = sb("xres", [P, BUFS, C], F32)
        y = sb("y", [P, C], F32)
        stats = sb("stats", [P, 6], F32)
        mv = sb("mv", [P, 2], F32)
        std = sb("std", [P, 1], F32)
        rstd = sb("rstd", [P, 1], F32)
        yo = sb("yo", [P, BUFS, C], F32)

        ps_group = [ps(f"ps_group{k}", [P, 512], F32) for k in range(2)]
        ps_count = ps("ps_count", [P, 4, 512], F32)
        ps_apply = ps("ps_apply", [P, 512], F32)
        ps_lin = ps("ps_lin", [P, 512], F32)
        CAT = 256
        acc_of_block = lambda b: bass.ds(b * P + MARGIN, P)

        edges_in = sem("edges_in")
        runs_in = sem("runs_in")
        tail_set = sem("tail_set")
        weights_in = sem("weights_in")
        x_in = [sem(f"x_in{c}") for c in range(NXCH)]
        iota_set = sem("iota_set")
        consts_set = sem("consts_set")
        pad_set = sem("pad_set")
        first_part = sem("first_part")
        rest_of_x = sem("rest_of_x")
        parts_done = sem("parts_done")
        xtab_out = sem("xtab_out")
        checked = sem("checked")
        starts_set = sem("starts_set")
        lined_in = sem("lined_in")
        windows_in = sem("windows_in")
        lined_cast = sem("lined_cast")
        turned = sem("turned")
        key_step = sem("key_step")
        tests_summed = sem("tests_summed")
        flag_set = sem("flag_set")
        gather_begun = sem("gather_begun")
        idx_ready = sem("idx_ready")
        rel_ready = sem("rel_ready")
        onehot_ready = sem("onehot_ready")
        gathered = [sem(f"gathered{k}") for k in range(SLOTS)]
        summed = sem("summed")
        added = sem("added")
        cleared = sem("cleared")
        keys_ready = sem("keys_ready")
        rowhot_ready = sem("rowhot_ready")
        hot_ready = sem("hot_ready")
        hot_used = sem("hot_used")
        counts_out = sem("counts_out")
        ctab_out = sem("ctab_out")
        ctab_in = sem("ctab_in")
        table_in = sem("table_in")
        applied_built = sem("applied_built")
        applied_loaded = sem("applied_loaded")
        squares_done = sem("squares_done")
        degree_done = sem("degree_done")
        rc_ready = sem("rc_ready")
        taken_step = [sem(f"taken_step{l}") for l in range(2)]
        linear_done = [sem(f"linear_done{l}") for l in range(2)]
        relu_done = sem("relu_done")
        split_step = sem("split_step")
        y_ready = sem("y_ready")
        norm_step = sem("norm_step")
        std_done = sem("std_done")
        stats_read = sem("stats_read")
        sp_held = sem("sp_held")
        h_out = [sem(f"h_out{k}") for k in range(BUFS)]
        y_out = [sem(f"y_out{k}") for k in range(BUFS)]
        res_in = [sem(f"res_in{k}") for k in range(BUFS)]

        block = ctx.enter_context(nc.Block())

        def tiles_of(g):
            return (TT, TP) if isinstance(g, int) and g == NG else (TILES, P)

        def gathers_before(layer, slot):
            n = 0
            for l in range(layer):
                n += sum(tiles_of(FIRST[l] + m)[0] for m in range(slot, GROUPS[l], SLOTS))
            return 16 * n

        def gathered_by(layer, i, step):
            slot = step % SLOTS
            if isinstance(i, int) and i * STEPS + step == GROUPS[layer] - 1:
                return gathers_before(layer + 1, slot)
            return i * (STEPS // SLOTS * TILES * 16) + ((step // SLOTS + 1) * TILES * 16 + gathers_before(layer, slot))

        def group_no(layer, i, step):
            return i * STEPS + (step + layer * (GROUPS[0] + BEYOND))

        def x_chunk(c):
            blocks = XCH if c < NXCH - 1 else 1
            return c * XCH, blocks, xin[:, c % 2, 0:blocks, :]

        @block.sync
        def _(sp):
            def hold(sem, value):
                wait(sp, sem, value)
                if not isinstance(value, int):
                    sp.sem_inc(sp_held, 1)

            for k, run in ((0, run0), (1, run1), (EXACT, run256)):
                sp.dma_start(run, edge_list[1, k:k + P * SORTED_COLS].rearrange("(p j) -> p j", p=P)).then_inc(runs_in, 16)
            def load_x(c):
                first, blocks, place = x_chunk(c)
                if c >= 2:
                    sp.wait_ge(parts_done, c - 1)
                if c < NXCH - 1:
                    rows = x[first * P:(first + blocks) * P, :].rearrange("(b p) c -> p b c", p=P)
                    sp.dma_start(place, rows).then_inc(x_in[c], 16)
                else:
                    sp.wait_ge(pad_set, 1)
                    sp.dma_start(place[0:LASTN, 0, :], x[first * P:N, :]).then_inc(x_in[c], 16)

            def store_x(c):
                first, blocks, _ = x_chunk(c)
                sp.wait_ge(parts_done, c + 1)
                sp.dma_start(xtab[first * P:(first + blocks) * P, :].rearrange("(b p) c -> p b c", p=P),
                             table[:, first:first + blocks, :]).then_inc(xtab_out, 16)

            load_x(0)
            sp.wait_ge(tail_set, 2)
            sp.dma_start(dst_all[:, 0:NG * TILES], dst_groups.rearrange("p g j -> p (g j)")).then_inc(edges_in, 16)
            sp.dma_start(dst_all[0:TP, NG * TILES:NG * TILES + TT], dst_tail).then_inc(edges_in, 16)
            load_x(1)
            sp.dma_start(idx_all[:, 0:NG * TILES], src_groups.rearrange("p g j -> p (g j)")).then_inc(edges_in, 16)
            sp.dma_start(idx_all[0:TP, NG * TILES:NG * TILES + TT], src_tail).then_inc(edges_in, 16)
            sp.dma_start(win, windows.rearrange("p (k n) -> p k n", k=2)).then_inc(windows_in, 16)
            sp.dma_start(unit[:], identity).then_inc(windows_in, 16)

            def load_lined(b):
                start = sp.value_load(starts[0:1, b:b + 1], min_val=0, max_val=E - P * CTILES)
                row = b % TURN * CTILES
                sp.dma_start(lined[row:row + CTILES, :, b // TURN, :],
                             edge_list[:, bass.ds(start, P * CTILES)].rearrange("k (t e) -> t k e", e=P)
                             ).then_inc(lined_in, 16)

            for c in range(NXCH):
                if c + 2 < NXCH:
                    load_x(c + 2)
                store_x(c)
                if c < KEYS_AT - 1:
                    sp.wait_ge(starts_set, 1)
                    for b in range(c, COUNTED[1], KEYS_AT - 1):
                        load_lined(b)
                if c == 0:
                    sp.dma_start(wt[:, 0, :], w1t).then_inc(weights_in, 16)
                    sp.dma_start(wt[:, 1, :], w2t).then_inc(weights_in, 16)
                    sp.dma_start(bias[:, 0, :], b1).then_inc(weights_in, 16)
                    sp.dma_start(bias[:, 1, :], b2).then_inc(weights_in, 16)

            def store_h(i, step):
                number, b, buf, _ = output(0, i, step)
                hold(split_step, number * 3 + 3)
                sp.dma_start(htab[bass.ds(b * P, P), :], hs[:, buf, :]).then_inc(h_out[buf], 16)

            def load_x_rows(i, step):
                number, b, buf, _ = output(1, i, step)
                hold(y_ready, number - 1)
                rows = LASTN if isinstance(b, int) and b == NB - 1 else P
                sp.dma_start(xres[0:rows, buf, :], x[bass.ds(b * P, rows), :]).then_inc(res_in[buf], 16)

            def store_y(i, step):
                number, b, buf, _ = output(1, i, step)
                hold(norm_step, number * 4 + 4)
                rows = LASTN if isinstance(b, int) and b == NB - 1 else P
                sp.dma_start(out[bass.ds(b * P, rows), :], yo[0:rows, buf, :]).then_inc(y_out[buf], 16)

            def all_h_stored(uses):
                for k in range(BUFS):
                    sp.wait_ge(h_out[k], 16 * uses[k])

            def all_y_stored(uses):
                for k in range(BUFS):
                    sp.wait_ge(y_out[k], 16 * uses[k])

            def fast():
                def round0(i):
                    first = isinstance(i, int) and i == 0
                    for step in OUTPUTS_FIRST[0] if first else OUTPUTS[0]:
                        store_h(i, step)
                        if step in (4, 8):
                            b = counted(0, i, step)
                            hold(counts_out, b * NPASS + NPASS)
                            sp.dma_start(ctab[bass.ds(b * P, P), :], built[:]).then_inc(ctab_out, 16)

                round0(0)
                with sp.Fori(1, ROUNDS[0]) as i:
                    round0(i)
                for step in OUTPUTS_LEFT[0]:
                    store_h(ROUNDS[0], step)
                all_h_stored([buffer_uses(0, k) for k in range(BUFS)])
                sp.wait_ge(applied_built, COUNTED[0])
                sp.dma_start(table[:], htab.rearrange("(b p) c -> p b c", p=P)).then_inc(table_in, 16)

                def load_counts(b):
                    hold(applied_loaded, b)
                    sp.wait_ge(ctab_out, 16 * COUNTED[0])
                    sp.dma_start(loaded[:], ctab[bass.ds(b * P, P), :]).then_inc(ctab_in, 16)

                def round1(i):
                    first = isinstance(i, int) and i == 0
                    steps = OUTPUTS_FIRST[1] if first else OUTPUTS[1]
                    for k, step in enumerate(steps):
                        if k + 1 < len(steps):
                            load_x_rows(i, steps[k + 1])
                        else:
                            load_x_rows(i + 1, OUTPUTS[1][0])
                        if step in ((3, 5) if first else (3,)):
                            load_counts(output(1, i, step)[1] + 1)
                        if step == 7:
                            b = output(1, i, step)[1] + 1
                            load_counts(b if first else i * 2 + 3)
                        store_y(i, step)

                load_counts(0)
                load_x_rows(0, OUTPUTS_FIRST[1][0])
                round1(0)
                with sp.Fori(1, ROUNDS[1]) as i:
                    round1(i)
                left = OUTPUTS_LEFT[1]
                for k, step in enumerate(left):
                    if k + 1 < len(left):
                        load_x_rows(ROUNDS[1], left[k + 1])
                    store_y(ROUNDS[1], step)
                sp.wait_ge(ctab_in, 16 * COUNTED[0])
                all_y_stored([buffer_uses(1, k) for k in range(BUFS)])

            def general():
                uses = [NB // BUFS + (k < NB % BUFS) for k in range(BUFS)]

                def one_h(b, buf):
                    hold(split_step, b * 3 + 3)
                    sp.dma_start(htab[bass.ds(b * P, P), :], hs[:, buf, :]).then_inc(h_out[buf], 16)

                def one_y(b, buf):
                    rows = LASTN if isinstance(b, int) and b == NB - 1 else P
                    hold(y_ready, b)
                    sp.dma_start(xres[0:rows, buf, :], x[bass.ds(b * P, rows), :]).then_inc(res_in[buf], 16)
                    hold(norm_step, b * 4 + 4)
                    sp.dma_start(out[bass.ds(b * P, rows), :], yo[0:rows, buf, :]).then_inc(y_out[buf], 16)

                for one in (one_h, one_y):
                    for k in range(BUFS):
                        one(k, k)
                    with sp.Fori(1, NB // BUFS) as r:
                        for k in range(BUFS):
                            one(r * BUFS + k, k)
                    for b in range(NB // BUFS * BUFS, NB):
                        one(b, b % BUFS)
                all_h_stored(uses)
                all_y_stored(uses)

            sp.wait_ge(flag_set, 2)
            violated = sp.value_load(flag[0:1, 0:1], min_val=0, max_val=1 << 14)
            with sp.If(violated):
                general()
            with sp.Else():
                fast()

        @block.gpsimd
        def _(pool):
            nc.gpsimd.memset(idx_all[:, NG * TILES:], 0).then_inc(tail_set, 1)
            nc.gpsimd.memset(dst_all[:, NG * TILES:], N - 1).then_inc(tail_set, 1)
            nc.gpsimd.memset(eps[:], EPS).then_inc(consts_set, 1)
            nc.gpsimd.memset(onesf[:], 1.0).then_inc(consts_set, 1)
            nc.gpsimd.memset(ones[:], 1.0).then_inc(consts_set, 1)
            nc.gpsimd.memset(zeros[:], 0.0).then_inc(consts_set, 1)
            nc.gpsimd.memset(keys_all[:, :, KEYCOLS:], -1.0).then_inc(consts_set, 1)
            nc.gpsimd.iota(base_all.rearrange("p (g j) -> p g j", j=TILES), [[SHARE, EDGEW // TILES], [0, TILES]],
                           base=-MARGIN, channel_multiplier=0).then_inc(iota_set, 1)
            nc.gpsimd.iota(nodes[:], [[1, NB * SPAN]], base=0, channel_multiplier=0).then_inc(iota_set, 1)
            pool.wait_ge(parts_done, NXCH - 2)
            nc.gpsimd.memset(x_chunk(NXCH - 1)[2], 0.0).then_inc(pad_set, 1)

            def gather(layer, g, slot, groups_done, h_uses):
                tiles, parts = tiles_of(g)
                if layer == 0:
                    pool.wait_ge(xtab_out, 16 * NXCH)
                else:
                    for k in range(BUFS):
                        pool.wait_ge(h_out[k], 16 * h_uses[k])
                pool.wait_ge(idx_ready, groups_done + 1)
                pool.sem_inc(gather_begun, 1)
                for j in range(tiles):
                    nc.gpsimd.indirect_dma_start(
                        out=msg[0:parts, slot, j, :], out_offset=None, in_=tables[layer],
                        in_offset=bass.IndirectOffsetOnAxis(ap=idx[0:parts, slot, j:j + 1], axis=0),
                    ).then_inc(gathered[slot], 16)

            def fast():
                uses = [buffer_uses(0, k) for k in range(BUFS)]
                for layer in range(2):
                    with pool.Fori(0, ROUNDS[layer]) as i:
                        for step in range(STEPS):
                            gather(layer, None, step % SLOTS, group_no(layer, i, step), uses)
                    for m in range(ROUNDS[layer] * STEPS, GROUPS[layer]):
                        gather(layer, FIRST[layer] + m, m % SLOTS, group_no(layer, 0, m), uses)

            def general():
                uses = [NB // BUFS + (k < NB % BUFS) for k in range(BUFS)]
                for layer in range(2):
                    with pool.Fori(0, NG) as g:
                        gather(layer, g, 0, g + layer * G, uses)
                    gather(layer, NG, 0, NG + layer * G, uses)

            pool.wait_ge(flag_set, 2)
            violated = pool.value_load(flag[0:1, 0:1], min_val=0, max_val=1 << 14)
            with pool.If(violated):
                general()
            with pool.Else():
                fast()

        @block.tensor
        def _(pe):
            pe.wait_ge(consts_set, 5)
            pe.wait_ge(checked, 6)
            pe.matmul(ps_lin[:, 1:1 + COUNTED[1]], onesf[:], tests[:, 1:], start=True, stop=True
                      ).then_inc(tests_summed, 1)
            pe.wait_ge(lined_cast, 2)
            pe.wait_ge(windows_in, 32)
            for k, bank in enumerate((ps_count[:, 0, :], ps_apply[:])):
                for g in range(NTURN):
                    tiles = min(TURN, COUNTED[1] - g * TURN) * CTILES
                    at = g * TURN * CTILES
                    mm = pe.matmul(bank[:, at:at + tiles], lined_f32[0:tiles, k, g, :], unit[0:tiles, 0:tiles],
                                   start=True, stop=True)
            mm.then_inc(turned, 1)
            pe.wait_ge(checked, 15)
            pe.matmul(ps_lin[:, 0:1], onesf[:], tests[:, 0:1], start=True, stop=True).then_inc(tests_summed, 1)
            pe.wait_ge(weights_in, 64)

            def sum_rows(sums, counts, rows, hot, tiles, parts, groups=1):
                for j in range(tiles):
                    for s in range(PARTS):
                        mm = pe.matmul(sums, rows[0:parts, j, s * C:(s + 1) * C], hot[0:parts, j, :],
                                       start=(j == 0 and s == 0), stop=(j == tiles - 1 and s == PARTS - 1))
                if counts is not None:
                    for j in range(tiles):
                        mm = pe.matmul(counts, ones[0:parts, :], hot[0:parts, j, :],
                                       start=(j == 0), stop=(j == tiles - 1))
                mm.then_inc(summed, groups)

            def linear(layer, number):
                pe.wait_ge(taken_step[layer], number * 2 + 2)
                if layer == 0:
                    wait(pe, relu_done, number * 2)
                else:
                    wait(pe, y_ready, number)
                pe.matmul(ps_lin[:, CAT:CAT + 1], taken[0:1, 1, :], onesf[0:1, 0:1], start=True, stop=True)
                pe.matmul(ps_lin[:, 0:C], taken[:, 0, :], wt[:, layer, :], start=True, stop=False)
                pe.matmul(ps_lin[:, 0:C], taken[0:1, 1, :], bias[:, layer, :], start=False, stop=True
                          ).then_inc(linear_done[layer], 1)

            def fast():
                for layer in range(2):
                    def group(i, step):
                        n = group_no(layer, i, step)
                        last = isinstance(i, int) and i * STEPS + step == GROUPS[layer] - 1
                        tiles, parts = tiles_of(NG) if last else (TILES, P)
                        bank = ps_group[step % 2]
                        pe.wait_ge(onehot_ready, n + 1)
                        pe.wait_ge(gathered[step % SLOTS], gathered_by(layer, i, step))
                        wait(pe, added, n - 1)
                        sum_rows(bank[:, 0:W], bank[:, CAT:CAT + W] if layer == 0 else None,
                                 msg[:, step % SLOTS], onehot[:, step % SLOTS], tiles, parts,
                                 groups=1 + BEYOND if last else 1)

                    def count_pass(d, p):
                        half = 2 * (p % 2)
                        wait(pe, counts_out, d * NPASS + (p - 1 if p else 0))
                        if p == 0:
                            pe.wait_ge(rowhot_ready, d + 1)
                        banks = [ps_count[:, half + k, 0:blocks * P] for k, (_, blocks) in enumerate(HALVES)]
                        for bank in banks:
                            pe.matmul(bank, zeros[:, 0:P], zeros[:, 0:bank.shape[1]], start=True, stop=False)
                        for c in range(CHUNKS):
                            q = p * CHUNKS + c
                            pe.wait_ge(hot_ready, d * NHOT + (q + 1))
                            for t in range(HOT_TILES):
                                tile = c * HOT_TILES + t
                                for (b, blocks), bank in zip(HALVES, banks):
                                    window = bank.rearrange("p (b n) -> p b n", n=P)[
                                        :, :, tile_first(tile, N * P // E):tile_first(tile, N * P // E) + SPAN]
                                    hot = colhot[:, q % HOT_BUFS, t, b * SPAN:(b + blocks) * SPAN]
                                    mm = pe.matmul(window, rowhot[:, tile, :], hot.rearrange("p (b n) -> p b n", n=SPAN),
                                                   start=False, stop=(tile == CTILES - 1))
                            mm.then_inc(hot_used, 1)

                    def apply(counts, blocks, applied):
                        for q in blocks:
                            columns = counts[:, q * P:(q + 1) * P]
                            for s in range(PARTS):
                                mm = pe.matmul(ps_apply[:, 0:C], table[:, q, s * C:(s + 1) * C], columns,
                                               start=(q == 0 and s == 0),
                                               stop=(layer == 1 and q == NB - 1 and s == PARTS - 1))
                            if layer == 0:
                                mm = pe.matmul(ps_apply[:, CAT:CAT + P], ones[:], columns,
                                               start=False, stop=(q == NB - 1))
                        if NB - 1 in blocks:
                            mm.then_inc(applied, 1)

                    def apply_pass(d, p):
                        pe.wait_ge(parts_done, NXCH)
                        pe.wait_ge(counts_out, d * NPASS + (p + 1))
                        apply(built, range(p * PASS_BLOCKS, (p + 1) * PASS_BLOCKS), applied_built)

                    def one_round(i):
                        first = isinstance(i, int) and i == 0
                        outputs = (OUTPUTS_FIRST if first else OUTPUTS)[layer]
                        for step in range(STEPS):
                            d = counted(layer, i, step)
                            group(i, step)
                            passes = PASSES[layer][step] if counts_at(layer, i) else ()
                            for p in passes:
                                count_pass(d, p)
                            if step in outputs:
                                linear(layer, output(layer, i, step)[0])
                            for p in APPLIED[layer][step]:
                                apply_pass(d, p)
                            if layer == 1 and step in ((2, 4, 6) if first else (2, 6)):
                                b = output(1, i, step + 1)[1]
                                if first and b == 0:
                                    pe.wait_ge(table_in, 16)
                                pe.wait_ge(ctab_in, b * 16 + 16)
                                apply(loaded, range(NB), applied_loaded)
                            if layer == 1 and step == 8:
                                pe.wait_ge(counts_out, d * NPASS + NPASS)
                                apply(built, range(NB), applied_built)

                    if layer == 1:
                        pe.wait_ge(relu_done, 2 * NB)
                    one_round(0)
                    with pe.Fori(1, ROUNDS[layer]) as i:
                        one_round(i)
                    i = ROUNDS[layer]
                    for step in range(LEFT[layer]):
                        group(i, step)
                        linear(layer, output(layer, i, step)[0])
                    for step in OUTPUTS_LEFT[layer][LEFT[layer]:]:
                        linear(layer, output(layer, i, step)[0])

            def general():
                for layer in range(2):
                    def chunk(n, c, tiles, parts, landed):
                        q = n * NCHUNK + c
                        pe.wait_ge(gathered[0], landed)
                        pe.wait_ge(onehot_ready, q + 1)
                        sum_rows(ps_group[0][:, 0:CHUNK], ps_group[1][:, 0:CHUNK], msg[:, 0], wide_onehot,
                                 tiles, parts)
                    with pe.Fori(0, NG) as g:
                        landed = (g + 1) * (16 * TILES) + layer * 16 * (NG * TILES + TT)
                        with pe.Fori(0, NCHUNK) as c:
                            chunk(g + layer * G, c, TILES, P, landed)
                    with pe.Fori(0, NCHUNK) as c:
                        chunk(NG + layer * G, c, TT, TP, (layer + 1) * 16 * (NG * TILES + TT))
                    if layer == 1:
                        pe.wait_ge(relu_done, 2 * NB)
                    linear(layer, 0)
                    with pe.Fori(1, NB) as b:
                        linear(layer, b)

            pe.wait_ge(flag_set, 2)
            violated = pe.value_load(flag[0:1, 0:1], min_val=0, max_val=1 << 14)
            with pe.If(violated):
                general()
            with pe.Else():
                fast()

        @block.scalar
        def _(act):
            for c in range(NXCH):
                first, blocks, place = x_chunk(c)
                act.wait_ge(x_in[c], 16)
                nc.scalar.activation(table[:, first:first + blocks, 0:C], place, ACT.Copy).then_inc(first_part, 1)
                act.wait_ge(rest_of_x, c + 1)
                nc.scalar.activation(table[:, first:first + blocks, C:2 * C], xrest[:, c % 2, 0:blocks, :],
                                     ACT.Copy).then_inc(first_part, 1)

            def take(layer, number, b, product=False):
                at = acc_of_block(b)
                wait(act, linear_done[layer], number)
                if not product:
                    nc.scalar.activation(taken[:], acc[:, :, at], ACT.Copy).then_inc(taken_step[layer], 2)
                    return
                found = ps_apply[:].rearrange("p (k n) -> p k n", k=2)[:, :, 0:P]
                if layer == 0:
                    nc.scalar.activation(taken[:], found, ACT.Copy).then_inc(taken_step[layer], 1)
                    nc.scalar.activation(cnt[:, at], found[:, 1, :], ACT.Copy).then_inc(taken_step[layer], 1)
                else:
                    nc.scalar.activation(taken[:, 0, :], found[:, 0, :], ACT.Copy).then_inc(taken_step[layer], 1)
                    nc.scalar.activation(taken[:, 1, :], cnt[:, at], ACT.Copy).then_inc(taken_step[layer], 1)

            def relu(number, buf, uses):
                act.wait_ge(rc_ready, number + 1)
                wait(act, split_step, number * 3)
                wait(act, h_out[buf], uses * 16)
                nc.scalar.activation(h32[:], ps_lin[:, 0:C], ACT.Relu, scale=rc[:, 0:1]).then_inc(relu_done, 1)
                nc.scalar.activation(hs[:, buf, 0:C], ps_lin[:, 0:C], ACT.Relu, scale=rc[:, 0:1]).then_inc(relu_done, 1)

            def deviation(number):
                act.wait_ge(norm_step, number * 4 + 2)
                nc.scalar.activation(std[:], mv[:, 1:2], ACT.Sqrt, bias=eps[:, 0:1]).then_inc(std_done, 1)

            def fast():
                for layer in range(2):
                    def keep_counts(d, p):
                        half = 2 * (p % 2)
                        if p == 0:
                            wait(act, applied_built, d + layer)
                            if layer == 0:
                                wait(act, ctab_out, d * 16)
                        act.wait_ge(hot_used, d * NHOT + (p + 1) * CHUNKS)
                        found = ps_count[:, half:half + 2, :].rearrange("p k n -> p (k n)")[:, 0:PASSW]
                        nc.scalar.activation(built[:, p * PASSW:(p + 1) * PASSW], found, ACT.Copy
                                             ).then_inc(counts_out, 1)

                    def one_hots(i, step):
                        n = group_no(layer, i, step)
                        hot = onehot[:, step % SLOTS]
                        act.wait_ge(idx_ready, n + 1)
                        for j in range(TILES):
                            op = nc.scalar.activation(hot[:, j, :], nodes[:, 0:W], ACT.Square,
                                                      bias=rel[:, step % SLOTS, j:j + 1])
                        op.then_inc(squares_done, 1)
                        act.wait_ge(squares_done, n + 1)
                        nc.scalar.activation(hot, hot, ACT.Relu, bias=onesf[:, 0:1], scale=-1.0).then_inc(onehot_ready, 1)

                    def begin(i, step, groups):
                        number, b, _, _ = output(layer, i, step)
                        if step % 2 == 0:
                            act.wait_ge(added, group_no(layer, i, groups))
                        elif layer == 0 or step == 1:
                            act.wait_ge(applied_built, b + (1 + layer))
                        else:
                            act.wait_ge(applied_loaded, b + 1)
                        take(layer, number, b, product=step % 2 == 1)

                    def end(i, step):
                        if layer == 0:
                            number, _, buf, uses = output(0, i, step)
                            relu(number, buf, uses)
                        else:
                            deviation(output(1, i, step)[0])

                    def one_round(i):
                        first = isinstance(i, int) and i == 0
                        outputs = (OUTPUTS_FIRST if first else OUTPUTS)[layer]
                        for step in range(STEPS):
                            if step - 1 in outputs:
                                end(i, step - 1)
                            if step in outputs:
                                begin(i, step, step)
                            one_hots(i, step + LEAD)
                            for p in PASSES[layer][step] if counts_at(layer, i) else ():
                                keep_counts(counted(layer, i, step), p)

                    if layer == 1:
                        act.wait_ge(relu_done, 2 * NB)
                    for step in range(LEAD):
                        one_hots(0, step)
                    one_round(0)
                    with act.Fori(1, ROUNDS[layer]) as i:
                        one_round(i)
                    i = ROUNDS[layer]
                    for step in OUTPUTS_LEFT[layer]:
                        begin(i, step, min(step, LEFT[layer]) if step in range(LEFT[layer]) else LEFT[layer])
                        end(i, step)

            def general():
                act.wait_ge(added, G * NCHUNK)
                for k in range(BUFS):
                    take(0, k, k)
                    relu(k, k, 0)
                with act.Fori(1, NB // BUFS) as r:
                    for k in range(BUFS):
                        take(0, r * BUFS + k, r * BUFS + k)
                        relu(r * BUFS + k, k, r)
                for b in range(NB // BUFS * BUFS, NB):
                    take(0, b, b)
                    relu(b, b % BUFS, NB // BUFS)
                act.wait_ge(added, 2 * G * NCHUNK)
                take(1, 0, 0)
                deviation(0)
                with act.Fori(1, NB) as b:
                    take(1, b, b)
                    deviation(b)

            act.wait_ge(flag_set, 2)
            violated = act.value_load(flag[0:1, 0:1], min_val=0, max_val=1 << 14)
            with act.If(violated):
                general()
            with act.Else():
                fast()

        @block.vector
        def _(dve):
            dve.wait_ge(runs_in, 48)
            nc.vector.tensor_tensor(order[:], run0, run1, ALU.is_gt).then_inc(checked, 1)
            dve.wait_ge(checked, 1)
            nc.vector.tensor_reduce(lim[:, 4:5], order[:], AX.X, ALU.max).then_inc(checked, 1)
            dve.wait_ge(checked, 2)
            nc.vector.tensor_tensor(order[:], run0, run256, ALU.is_equal).then_inc(checked, 1)
            dve.wait_ge(checked, 3)
            nc.vector.tensor_reduce(lim[:, 5:6], order[:], AX.X, ALU.max).then_inc(checked, 1)
            dve.wait_ge(checked, 4)
            nc.vector.tensor_copy(order[:], run0).then_inc(checked, 1)
            dve.wait_ge(checked, 5)
            for b in range(1, COUNTED[1] + 1):
                last = nc.vector.tensor_scalar(before[:, b - 1, :], order[:], float(b * P), None, ALU.is_lt, ALU.add,
                                               accum_out=tests[:, b:b + 1])
            last.then_inc(checked, 1)
            nc.vector.memset(sums[:, 0:1], 0.0).then_inc(cleared, 1)
            dve.wait_ge(tests_summed, 1)
            dve.wait_ge(cleared, 1)
            nc.vector.tensor_copy(sums[:, 1:], ps_lin[:, 1:1 + COUNTED[1]]).then_inc(checked, 1)
            dve.wait_ge(checked, 7)
            nc.vector.tensor_copy(starts[:], sums[:]).then_inc(starts_set, 1)
            nc.vector.tensor_tensor(span[:], sums[:, 1:1 + COUNTED[1]], sums[:, 0:COUNTED[1]], ALU.subtract
                                    ).then_inc(checked, 1)
            dve.wait_ge(checked, 8)
            nc.vector.tensor_reduce(lim[:, 8:9], span[:], AX.X, ALU.max).then_inc(checked, 1)
            dve.wait_ge(checked, 9)
            nc.vector.tensor_scalar(lim[:, 6:7], lim[:, 8:9], P * CTILES + 0.5, None, ALU.is_gt).then_inc(checked, 1)
            dve.wait_ge(edges_in, 64)
            dve.wait_ge(iota_set, 2)
            nc.vector.tensor_tensor(rel_all, base_all, dst_all[:], ALU.subtract).then_inc(checked, 1)
            dve.wait_ge(checked, 11)
            nc.vector.tensor_reduce(lim[:, 0:1], rel_all[:, 0:G * TILES], AX.X, ALU.min).then_inc(checked, 1)
            nc.vector.tensor_reduce(lim[:, 1:2], rel_all[:, 0:G * TILES], AX.X, ALU.max).then_inc(checked, 1)

            def split_x(c):
                first, blocks, place = x_chunk(c)
                rest = xrest[:, c % 2, 0:blocks, :]
                dve.wait_ge(first_part, 2 * c + 1)
                nc.vector.tensor_tensor(rest, place, table[:, first:first + blocks, 0:C], ALU.subtract
                                        ).then_inc(rest_of_x, 1)
                dve.wait_ge(rest_of_x, c + 1)
                dve.wait_ge(first_part, 2 * c + 2)
                nc.vector.tensor_tensor(table[:, first:first + blocks, 2 * C:3 * C], rest,
                                        table[:, first:first + blocks, C:2 * C], ALU.subtract
                                        ).then_inc(parts_done, 1)

            for c in range(KEYS_AT):
                split_x(c)
            dve.wait_ge(lined_in, 16 * COUNTED[1])
            full = COUNTED[1] // TURN
            rest = (COUNTED[1] - full * TURN) * CTILES
            nc.vector.tensor_copy(lined_f32[0:TURN * CTILES, :, 0:full, :], lined[0:TURN * CTILES, :, 0:full, :]
                                  ).then_inc(lined_cast, 1)
            nc.vector.tensor_copy(lined_f32[0:rest, :, full, :], lined[0:rest, :, full, :]).then_inc(lined_cast, 1)
            dve.wait_ge(turned, 1)
            dve.wait_ge(windows_in, 32)
            src_of, dst_of = ps_count[:, 0, 0:KEYCOLS], ps_apply[:, 0:KEYCOLS]
            nc.vector.tensor_copy(source, src_of).then_inc(key_step, 1)
            nc.vector.tensor_tensor(from_window, dst_of, win[:, 0, :], ALU.subtract).then_inc(key_step, 1)
            nc.vector.tensor_tensor(in_block, dst_of, win[:, 1, :], ALU.is_lt).then_inc(key_step, 1)
            dve.wait_ge(key_step, 3)
            nc.vector.tensor_scalar(low, source, P - 1, None, ALU.bitwise_and).then_inc(key_step, 1)
            nc.vector.tensor_scalar(not_before, from_window, 0.0, None, ALU.is_ge).then_inc(key_step, 1)
            dve.wait_ge(key_step, 5)
            nc.vector.tensor_copy(keys_all[:, 0, 0:KEYCOLS], low).then_inc(key_step, 1)
            nc.vector.scalar_tensor_tensor(out=inside, in0=from_window, scalar=float(SPAN), in1=not_before,
                                           op0=ALU.is_lt, op1=ALU.mult).then_inc(key_step, 1)
            dve.wait_ge(key_step, 7)
            nc.vector.tensor_tensor(from_block, src_of, keys_all[:, 0, 0:KEYCOLS], ALU.subtract).then_inc(key_step, 1)
            nc.vector.tensor_tensor(outside, in_block, inside, ALU.subtract).then_inc(key_step, 1)
            dve.wait_ge(key_step, 9)
            nc.vector.scalar_tensor_tensor(out=column, in0=from_block, scalar=SPAN / P, in1=from_window,
                                           op0=ALU.mult, op1=ALU.add).then_inc(key_step, 1)
            nc.vector.tensor_reduce(lim[:, 7:8], outside, AX.X, ALU.max).then_inc(key_step, 1)
            dve.wait_ge(key_step, 11)
            nc.vector.scalar_tensor_tensor(out=column1, in0=column, scalar=1.0, in1=inside,
                                           op0=ALU.add, op1=ALU.mult).then_inc(key_step, 1)
            dve.wait_ge(key_step, 12)
            nc.vector.tensor_scalar(keys_all[:, 1, 0:KEYCOLS], column1, -1.0, None, ALU.add).then_inc(key_step, 1)
            dve.wait_ge(checked, 13)
            nc.vector.tensor_scalar(lim[:, 2:3], lim[:, 0:1], 0.5 - W, None, ALU.is_lt).then_inc(checked, 1)
            nc.vector.tensor_scalar(lim[:, 3:4], lim[:, 1:2], 0.5, None, ALU.is_gt).then_inc(key_step, 1)
            dve.wait_ge(checked, 14)
            dve.wait_ge(key_step, 14)
            nc.vector.tensor_reduce(tests[:, 0:1], lim[:, 2:8], AX.X, ALU.max).then_inc(checked, 1)
            dve.wait_ge(tests_summed, 2)
            nc.vector.tensor_copy(flag[:], ps_lin[:, 0:1]).then_inc(flag_set, 2)
            for c in range(KEYS_AT, NXCH):
                split_x(c)

            def degrees(layer, number):
                n = number + layer * NB
                dve.wait_ge(linear_done[layer], number + 1)
                nc.vector.tensor_scalar(degree[:], ps_lin[:, CAT:CAT + 1], 1.0, None, ALU.max).then_inc(degree_done, 1)
                dve.wait_ge(degree_done, n + 1)
                nc.vector.reciprocal(rc[:, layer:layer + 1], degree[:]).then_inc(rc_ready, 1)

            def split_h(number, buf):
                n = number * 3
                dve.wait_ge(relu_done, number * 2 + 2)
                nc.vector.tensor_tensor(hr[:], h32[:], hs[:, buf, 0:C], ALU.subtract).then_inc(split_step, 1)
                dve.wait_ge(split_step, n + 1)
                nc.vector.tensor_copy(hs[:, buf, C:2 * C], hr[:]).then_inc(split_step, 1)
                dve.wait_ge(split_step, n + 2)
                nc.vector.tensor_tensor(hs[:, buf, 2 * C:3 * C], hr[:], hs[:, buf, C:2 * C],
                                        ALU.subtract).then_inc(split_step, 1)

            def residual(number, b, buf, uses):
                n = number * 4
                rows = LASTN if isinstance(b, int) and b == NB - 1 else P
                dve.wait_ge(rc_ready, number + (NB + 1))
                wait(dve, norm_step, n)
                dve.wait_ge(res_in[buf], uses * 16 + 16)
                nc.vector.scalar_tensor_tensor(out=y[0:rows, :], in0=ps_lin[0:rows, 0:C], scalar=rc[0:rows, 1:2],
                                               in1=xres[0:rows, buf, :], op0=ALU.mult, op1=ALU.add
                                               ).then_inc(y_ready, 1)
                dve.wait_ge(y_ready, number + 1)
                nc.vector.bn_stats(stats[:], y[:]).then_inc(norm_step, 1)
                dve.wait_ge(norm_step, n + 1)
                dve.sem_inc(stats_read, 1)
                nc.vector.bn_aggr(mv[:], stats[:]).then_inc(norm_step, 1)

            def norm(number, buf, uses):
                n = number * 4
                dve.wait_ge(std_done, number + 1)
                nc.vector.reciprocal(rstd[:], std[:]).then_inc(norm_step, 1)
                dve.wait_ge(norm_step, n + 3)
                wait(dve, y_out[buf], uses * 16)
                nc.vector.tensor_scalar(yo[:, buf, :], y[:], mv[:, 0:1], rstd[:, 0:1],
                                        ALU.subtract, ALU.mult).then_inc(norm_step, 1)

            def fast():
                def block_keys(d):
                    wait(dve, hot_ready, d * NHOT)
                    nc.vector.tensor_copy(keys[:], keys_all[:, :, bass.ds(d * CTILES, CTILES)]).then_inc(keys_ready, 1)

                def row_rows(d):
                    wait(dve, hot_used, d * NHOT)
                    for t in range(CTILES):
                        op = nc.vector.tensor_scalar(rowhot[:, t, :], nodes[:, 0:P], keys[:, 0, t:t + 1], None,
                                                     ALU.is_equal)
                    op.then_inc(rowhot_ready, 1)

                def hot_rows(d, p):
                    if p == 0:
                        dve.wait_ge(keys_ready, d + 1)
                    for c in range(CHUNKS):
                        q = p * CHUNKS + c
                        wait(dve, hot_used, d * NHOT + (q + 1 - HOT_BUFS))
                        for t in range(HOT_TILES):
                            tile = c * HOT_TILES + t
                            op = nc.vector.tensor_scalar(colhot[:, q % HOT_BUFS, t, :], nodes[:, p * HOTW:(p + 1) * HOTW],
                                                         keys[:, 1, tile:tile + 1], None, ALU.is_equal)
                        op.then_inc(hot_ready, 1)

                for layer in range(2):
                    def prepare(i, step):
                        n = group_no(layer, i, step)
                        slot = step % SLOTS
                        wait(dve, summed, n - (SLOTS - 1))
                        at = bass.ds((i * STEPS + (step + FIRST[layer])) * (2 * TILES), 2 * TILES)
                        nc.vector.tensor_copy(edges[:, slot].bitcast(I16), edges_all[:].bitcast(I16)[:, :, at]
                                              ).then_inc(idx_ready, 1)

                    def evacuate(i, step):
                        n = group_no(layer, i, step)
                        kinds = 2 if layer == 0 else 1
                        bank = ps_group[step % 2][:].rearrange("p (k n) -> p k n", k=2)[:, 0:kinds, :]
                        dve.wait_ge(summed, n + 1)
                        wait(dve, added, n)
                        at = (i * STEPS + (step + FIRST[layer])) * SHARE
                        old, new = bass.ds(at, OLD), bass.ds(at + OLD, SHARE)
                        nc.vector.tensor_tensor(acc[:, 0:kinds, old], acc[:, 0:kinds, old], bank[:, :, 0:OLD], ALU.add)
                        last = isinstance(i, int) and i * STEPS + step == GROUPS[layer] - 1
                        nc.vector.tensor_copy(acc[:, 0:kinds, new], bank[:, :, OLD:W]
                                              ).then_inc(added, 1 + BEYOND if last else 1)

                    def begin(i, step):
                        number, b, buf, uses = output(layer, i, step)
                        degrees(layer, number)
                        if layer == 1:
                            residual(number, b, buf, uses)

                    def end(i, step):
                        number, b, buf, uses = output(layer, i, step)
                        if layer == 0:
                            split_h(number, buf)
                        else:
                            norm(number, buf, uses)

                    def one_round(i):
                        first = isinstance(i, int) and i == 0
                        outputs = (OUTPUTS_FIRST if first else OUTPUTS)[layer]
                        for step in range(STEPS):
                            prepare(i, step + LEAD)
                            if step:
                                evacuate(i, step - 1)
                            elif not first:
                                evacuate(i - 1, STEPS - 1)
                            if step - 2 in outputs:
                                end(i, step - 2)
                            if step == 0 and not first:
                                end(i - 1, STEPS - 2)
                            if step - 1 in outputs:
                                begin(i, step - 1)
                            d = counted(layer, i, step)
                            if counts_at(layer, i):
                                for p in PASSES[layer][step]:
                                    if p + 2 < NPASS:
                                        hot_rows(d, p + 2)
                                if step in ((3, 8) if layer == 0 else (6,)):
                                    block_keys(d + 1)
                                    hot_rows(d + 1, 0)
                                if step in ((4, 9) if layer == 0 else (7,)):
                                    row_rows(d + 1)
                                    hot_rows(d + 1, 1)

                    first_old = slice(FIRST[layer] * SHARE, FIRST[layer] * SHARE + OLD)
                    if layer == 0:
                        nc.vector.memset(cnt[:, first_old], 0.0).then_inc(cleared, 1)
                    nc.vector.memset(agg[:, first_old], 0.0).then_inc(cleared, 1)
                    dve.wait_ge(cleared, 3 + layer)
                    if layer == 0:
                        dve.wait_ge(consts_set, 5)
                        block_keys(0)
                        hot_rows(0, 0)
                        row_rows(0)
                        hot_rows(0, 1)
                    else:
                        dve.wait_ge(onehot_ready, GROUPS[0] + BEYOND)
                    for step in range(LEAD):
                        prepare(0, step)
                    one_round(0)
                    with dve.Fori(1, ROUNDS[layer]) as i:
                        one_round(i)
                    i = ROUNDS[layer]
                    for step in range(LEFT[layer]):
                        if step:
                            evacuate(i, step - 1)
                            begin(i, step - 1)
                            end(i, step - 1)
                        else:
                            evacuate(i - 1, STEPS - 1)
                            end(i - 1, STEPS - 2)
                    evacuate(i, LEFT[layer] - 1)
                    for step in OUTPUTS_LEFT[layer][LEFT[layer] - 1:]:
                        begin(i, step)
                        end(i, step)

            def general():
                for layer in range(2):
                    def all_chunks(column, n):
                        at = bass.ds(column, TILES)
                        nc.vector.tensor_copy(idx[:, 0, :], idx_all[:, at]).then_inc(idx_ready, 1)
                        wait(dve, rel_ready, n * (NCHUNK + 1))
                        nc.vector.tensor_copy(rel[:, 0, :], dst_all[:, at]).then_inc(rel_ready, 1)
                        with dve.Fori(0, NCHUNK) as c:
                            q = n * NCHUNK + c
                            dve.wait_ge(rel_ready, n * (NCHUNK + 1) + c + 1)
                            for j in range(TILES):
                                op = nc.vector.tensor_scalar(wide_onehot[:, j, :], nodes[:, 0:CHUNK],
                                                             rel[:, 0, j:j + 1], None, ALU.is_equal)
                            op.then_inc(onehot_ready, 1)
                            dve.wait_ge(summed, q + 1)
                            at = bass.ds(c * CHUNK + MARGIN, CHUNK)
                            if layer == 0:
                                nc.vector.tensor_tensor(cnt[:, at], cnt[:, at], ps_group[1][:, 0:CHUNK], ALU.add)
                            nc.vector.tensor_tensor(agg[:, at], agg[:, at], ps_group[0][:, 0:CHUNK], ALU.add
                                                    ).then_inc(added, 1)
                            dve.wait_ge(added, q + 1)
                            nc.vector.tensor_scalar(rel[:, 0, :], rel[:, 0, :], float(-CHUNK), None, ALU.add
                                                    ).then_inc(rel_ready, 1)

                    if layer == 0:
                        nc.vector.memset(cnt, 0.0).then_inc(cleared, 1)
                    nc.vector.memset(agg, 0.0).then_inc(cleared, 1)
                    dve.wait_ge(cleared, 3 + layer)
                    all_chunks(0, layer * G)
                    with dve.Fori(1, NG) as g:
                        all_chunks(g * TILES, g + layer * G)
                    all_chunks(NG * TILES, NG + layer * G)

                    def one(b, buf, uses):
                        degrees(layer, b)
                        if layer == 0:
                            split_h(b, buf)
                        else:
                            residual(b, b, buf, uses)
                            norm(b, buf, uses)
                    for k in range(BUFS):
                        one(k, k, 0)
                    with dve.Fori(1, NB // BUFS) as r:
                        for k in range(BUFS):
                            one(r * BUFS + k, k, r)
                    for b in range(NB // BUFS * BUFS, NB):
                        one(b, b % BUFS, NB // BUFS)

            dve.wait_ge(flag_set, 2)
            violated = dve.value_load(flag[0:1, 0:1], min_val=0, max_val=1 << 14)
            with dve.If(violated):
                general()
            with dve.Else():
                fast()


def kernel(x, src, dst, L0_gnn_W1, L0_gnn_b1, L0_gnn_W2, L0_gnn_b2):
    import numpy as _np
    import concourse.bacc as _bacc
    from concourse import mybir as _mybir
    from concourse.bass_utils import run_bass_kernel_spmd as _run

    src, dst = _np.asarray(src), _np.asarray(dst)
    full = src.shape[0] // GROUP_EDGES
    tiles, parts = split_of_tail(src.shape[0] - full * GROUP_EDGES)

    def groups(e):
        return _np.ascontiguousarray(e[:full * GROUP_EDGES].reshape(full, P, TILES).transpose(1, 0, 2))

    def tail(e):
        return _np.ascontiguousarray(e[full * GROUP_EDGES:].reshape(parts, tiles))

    arrays = {
        "x": _np.ascontiguousarray(x),
        "edge_list": _np.stack([src, dst]),
        "src_groups": groups(src), "dst_groups": groups(dst),
        "src_tail": tail(src), "dst_tail": tail(dst),
        "w1t": _np.ascontiguousarray(_np.asarray(L0_gnn_W1).T), "b1": _np.asarray(L0_gnn_b1).reshape(1, -1),
        "w2t": _np.ascontiguousarray(_np.asarray(L0_gnn_W2).T), "b2": _np.asarray(L0_gnn_b2).reshape(1, -1),
    }
    blocks = _np.repeat(_np.arange(COUNTED[1]) * P, CTILES)
    firsts = _np.tile([tile_first(t, x.shape[0] * P // src.shape[0]) for t in range(CTILES)], COUNTED[1])
    windows = _np.concatenate([blocks + firsts, blocks + P]).astype(_np.float32)
    arrays["windows"] = _np.ascontiguousarray(_np.broadcast_to(windows, (P, windows.size)))
    arrays["identity"] = _np.eye(P, dtype=_np.float32)
    nc = _bacc.Bacc("TRN2", target_bir_lowering=False, num_devices=1)
    args = [nc.dram_tensor(n, a.shape, _mybir.dt.from_np(a.dtype), kind="ExternalInput").ap()
            for n, a in arrays.items()]
    args.append(nc.dram_tensor("out", x.shape, _mybir.dt.from_np(arrays["x"].dtype), kind="ExternalOutput").ap())
    gnn_resnorm(nc, *args)
    return _run(nc, [arrays], core_ids=[0]).results[0]["out"]
```

```python
from contextlib import ExitStack

import concourse.bass as bass
from concourse import mybir

P = 128
ALU = mybir.AluOpType
ACT = mybir.ActivationFunctionType
AX = mybir.AxisListType
F32 = mybir.dt.float32
BF16 = mybir.dt.bfloat16
I32 = mybir.dt.int32
I16 = mybir.dt.int16

EPS = 1e-5
TILES = 8
GROUP_EDGES = TILES * P
MARGIN = 40
SLOTS = 5
PARTS = 3
STEPS = 10
COUNTED = (14, 22)
CTILES = 18
PASS_BLOCKS = 7
SPAN = 32
HOT_TILES = 6
HOT_BUFS = 7
EXACT = 256
SORTED_COLS = 360
BUFS = 3
LINED_BY_SP = 10
CAST_AT = 4
LEAD = 3


def split_of_tail(edges):
    for tiles in range(1, edges + 1):
        if edges % tiles == 0 and edges // tiles <= P:
            return tiles, edges // tiles


def wait(eng, sem, value):
    if not (isinstance(value, int) and value <= 0):
        eng.wait_ge(sem, value)


def tile_first(t, share):
    return min(max(t * share + share // 2 - SPAN // 2, 0), P - SPAN)


def tile_order(share):
    order, covered = [(0, 0)], SPAN
    while covered < P:
        t = max(t for t in range(CTILES) if tile_first(t, share) <= covered)
        order.append((t, covered))
        covered = tile_first(t, share) + SPAN
    taken = [t for t, _ in order]
    return order + [(t, P) for t in range(CTILES) if t not in taken]


def gnn_resnorm(nc, x, edge_list, src_groups, dst_groups, src_tail, dst_tail, w1t, b1, w2t, b2,
                windows, identity, out):
    N, C = x.shape
    NG = src_groups.shape[1]
    E = edge_list.shape[1]
    TT, TP = src_tail.shape[1], src_tail.shape[0]
    G = NG + 1
    NB = -(-N // P)
    LASTN = N - (NB - 1) * P
    SHARE = N * GROUP_EDGES // E
    W = SHARE + 2 * MARGIN
    OLD = W - SHARE
    ROW = PARTS * C
    AGGW = NB * P + 2 * MARGIN + SHARE
    CHUNK = 448
    NCHUNK = NB * P // CHUNK
    XBUFS = 4
    XCH = 8
    NXCH = NB // XCH + 1
    ROUNDS = (COUNTED[0] // 2, (COUNTED[1] - COUNTED[0]) // 2 + 1)
    FIRST = tuple(2 * k - 1 for k in COUNTED)
    LEFT = tuple(G - f - STEPS * r for f, r in zip(FIRST, ROUNDS))
    BEYOND = LEAD - 1
    GROUPS = tuple(G - f for f in FIRST)
    TILE_SHARE = N * P // E
    ORDER = tile_order(TILE_SHARE)
    NPASS = NB // PASS_BLOCKS
    PASSW = PASS_BLOCKS * P
    HALVES = ((0, 4), (4, PASS_BLOCKS - 4))
    HOTW = PASS_BLOCKS * SPAN
    KEYCOLS = COUNTED[1] * CTILES
    TURN = P // CTILES
    NTURN = -(-COUNTED[1] // TURN)
    CHUNKS = CTILES // HOT_TILES
    NHOT = NPASS * CHUNKS
    assert C == P and SHARE * E == N * GROUP_EDGES and NCHUNK * CHUNK == NB * P and (NB - 1) % XCH == 0
    assert 2 * SHARE == P and MARGIN <= SHARE and NPASS * PASS_BLOCKS == NB
    EDGEW = (G + BEYOND) * TILES
    assert LEFT == (1, 5) and 2 * ROUNDS[0] == COUNTED[0] and COUNTED[0] - 1 == 3 + 2 * (ROUNDS[1] - 1) + 2
    assert 2 * (ROUNDS[1] - 1) == COUNTED[1] - COUNTED[0]
    assert HOT_BUFS >= 2 * CHUNKS and KEYCOLS <= 512 and STEPS % SLOTS == 0 and STEPS % 2 == 0 and NHOT % HOT_BUFS == 0
    assert SORTED_COLS * P >= ((COUNTED[1] * P + MARGIN) // SHARE + 1) * GROUP_EDGES

    OUTPUTS = ((0, 1, 2, 4, 5, 6, 8), (0, 1, 2, 3, 4, 5, 6, 7, 8))
    OUTPUTS_FIRST = ((4, 5, 6, 8), (3, 4, 5, 6, 7, 8))
    OUTPUTS_LEFT = ((0, 1, 2), (0, 1, 2, 3, 4, 5, 6))

    BEFORE_LAST = (2, 4)

    def from_dram(layer, i, step):
        return layer == 1 and (step in (3, 7) or (step == 5 and isinstance(i, int) and i in (0, ROUNDS[1])))

    def buffers(layer):
        count = len(OUTPUTS[layer])
        later = [1 if j == count - 1 and j % BUFS == 0 else j % BUFS for j in range(count)]
        return later[count - len(OUTPUTS_FIRST[layer]):], later, later[:len(OUTPUTS_LEFT[layer])]

    def output(layer, i, step):
        first, later, left = buffers(layer)
        if isinstance(i, int) and i == 0:
            j = OUTPUTS_FIRST[layer].index(step)
            buf = first[j]
            number, uses = j, first[:j].count(buf)
        else:
            last = isinstance(i, int) and i == ROUNDS[layer]
            j = (OUTPUTS_LEFT if last else OUTPUTS)[layer].index(step)
            buf = later[j]
            number = (i - 1) * len(later) + (len(first) + j)
            uses = (i - 1) * later.count(buf) + (first.count(buf) + later[:j].count(buf))
        if step % 2 == 0:
            block = i * (STEPS // 2) + (COUNTED[layer] - 2 + step // 2)
        elif not from_dram(layer, i, step):
            block = i * 2 + ((COUNTED[0] - 2) * layer + (-1 if step == 1 else 0))
        elif isinstance(i, int) and i == 0:
            block = (step - 3) // 2
        else:
            block = i * 2 + (1 if step == 3 else 2)
        return number, block, buf, uses

    def buffer_uses(layer, buf):
        per = [order.count(buf) for order in buffers(layer)]
        return per[0] + per[1] * (ROUNDS[layer] - 1) + per[2]

    PASSES = (((0,), (1, 2), (3, 4), (5, 6), ()) * 2,
              ((0, 1), (2, 3), (), (4, 5), (6,), (0, 1), (), (2, 3), (4, 5), (6,)))
    STORED = ((0, 4), (4, NPASS))
    APPLIED = (((), (0,), (1, 2), (3, 4), (5, 6)) * 2, ((), (), (), (), tuple(range(NPASS))) * 2)

    def counted(layer, i, step):
        return i * 2 + (step // 5 + (COUNTED[0] - 2) * layer)

    def counts_at(layer, i):
        return not (layer == 1 and isinstance(i, int) and i == 0)

    with ExitStack() as ctx:
        def sb(name, shape, dt):
            return ctx.enter_context(nc.sbuf_tensor(name, shape, dt))

        def ps(name, shape, dt):
            return ctx.enter_context(nc.psum_tensor(name, shape, dt))

        def sem(name):
            return ctx.enter_context(nc.semaphore(name))

        xtab = nc.dram_tensor("xtab", (NB * P, ROW), BF16).ap()
        htab = nc.dram_tensor("htab", (NB * P, ROW), BF16).ap()
        ctab = nc.dram_tensor("ctab", (COUNTED[0] * P, NB * P), BF16).ap()
        tables = [xtab, htab]

        table = sb("table", [P, NB, ROW], BF16)
        edges_all = sb("edges_all", [P, 2, EDGEW], I32)
        idx_all = edges_all[:, 0, :]
        dst_all = sb("dst_all", [P, EDGEW], I32)
        base_all = edges_all[:, 1, :]
        rel_all = base_all.bitcast(F32)
        acc = sb("acc", [P, 2, AGGW], F32)
        agg = acc[:, 0, :]
        cnt = acc[:, 1, :]
        nodes = sb("nodes", [P, NB * SPAN], I16)
        msg = sb("msg", [P, SLOTS, TILES, ROW], BF16)
        onehot = sb("onehot", [P, SLOTS, TILES, W], BF16)
        edges = sb("edges", [P, SLOTS, 2, TILES], I32)
        idx = edges[:, :, 0, :]
        rel = edges[:].bitcast(F32)[:, :, 1, :]
        built = sb("built", [P, NB * P], BF16)
        loaded = sb("loaded", [P, NB * P], BF16)
        wide_onehot = built[:, 0:TILES * CHUNK].rearrange("p (j n) -> p j n", j=TILES)
        keys_all = sb("keys_all", [P, 2, KEYCOLS + CTILES], F32)
        keys = sb("keys", [P, 2, CTILES], F32)
        rowhot = sb("rowhot", [P, CTILES, P], BF16)
        colhot = sb("colhot", [P, HOT_BUFS, HOT_TILES, HOTW], BF16)
        xin = colhot[:].rearrange("p k t n -> p (k t n)").bitcast(F32)[:, 0:XBUFS * XCH * C].rearrange(
            "p (k b c) -> p k b c", k=XBUFS, b=XCH)
        xrest = loaded[:].bitcast(F32)[:, 0:2 * XCH * C].rearrange("p (k b c) -> p k b c", k=2, b=XCH)
        scratch = msg[:].rearrange("p k t n -> p (k t n)").bitcast(F32)
        used = [0]

        def at_start(*shape):
            size = 1
            for n in shape:
                size *= n
            place = scratch[:, used[0]:used[0] + size]
            used[0] += size
            assert used[0] <= SLOTS * TILES * ROW // 2
            if len(shape) == 1:
                return place
            names = "abc"[:len(shape)]
            return place.rearrange(f"p ({' '.join(names)}) -> p {' '.join(names)}", **dict(zip(names, shape)))
        run0 = at_start(SORTED_COLS).bitcast(I32)
        first_used = used[0]
        run1, run256 = [at_start(SORTED_COLS).bitcast(I32) for k in range(2)]
        order = at_start(SORTED_COLS)
        lined = scratch[:, first_used:first_used + 2 * NTURN * P].bitcast(I32).rearrange(
            "p (k g e) -> p k g e", k=2, g=NTURN)
        short = at_start(SORTED_COLS // 2).bitcast(I16)
        win = at_start(2, KEYCOLS)
        lined_f32 = at_start(2, NTURN, P)
        before = scratch[:, used[0]:used[0] + COUNTED[1] * SORTED_COLS // 2].bitcast(BF16).rearrange(
            "p (b j) -> p b j", b=COUNTED[1])
        source, low = [at_start(KEYCOLS).bitcast(I32) for k in range(2)]
        from_block, from_window, not_before, inside, in_block, outside, column, column1 = [
            at_start(KEYCOLS) for k in range(8)]
        ones = sb("ones", [P, P], BF16)
        onesf = sb("onesf", [P, P], F32)
        unit = sb("unit", [P, P], F32)
        wt = sb("wt", [P, 2, C], F32)
        bias = sb("bias", [1, 2, C], F32)
        lim = sb("lim", [P, 9], F32)
        tests = sb("tests", [P, 1 + COUNTED[1]], F32)
        sums = sb("sums", [P, 1 + COUNTED[1]], F32)
        span = sb("span", [P, COUNTED[1]], F32)
        starts = sb("starts", [P, 1 + COUNTED[1]], I32)
        flag = sb("flag", [P, 1], I32)
        eps = sb("eps", [P, 1], F32)
        taken = sb("taken", [P, 2, C], F32)
        degree = sb("degree", [P, 1], F32)
        rc = sb("rc", [P, 2], F32)
        h32 = sb("h32", [P, C], F32)
        hr = sb("hr", [P, C], F32)
        hs = sb("hs", [P, BUFS, ROW], BF16)
        xres = sb("xres", [P, BUFS, C], F32)
        y = sb("y", [P, C], F32)
        stats = sb("stats", [P, 6], F32)
        mv = sb("mv", [P, 2], F32)
        std = sb("std", [P, 1], F32)
        rstd = sb("rstd", [P, 1], F32)
        yo = sb("yo", [P, BUFS, C], F32)

        ps_group = [ps(f"ps_group{k}", [P, 512], F32) for k in range(2)]
        ps_count = ps("ps_count", [P, 4, 512], F32)
        ps_apply = ps("ps_apply", [P, 512], F32)
        ps_lin = ps("ps_lin", [P, 512], F32)
        CAT = 256

        edges_in = sem("edges_in")
        runs_in = sem("runs_in")
        tail_set = sem("tail_set")
        weights_in = sem("weights_in")
        x_in = [sem(f"x_in{c}") for c in range(NXCH)]
        iota_set = sem("iota_set")
        consts_set = sem("consts_set")
        pad_set = sem("pad_set")
        first_part = sem("first_part")
        second_part = sem("second_part")
        rest_of_x = sem("rest_of_x")
        parts_done = sem("parts_done")
        xtab_out = sem("xtab_out")
        checked = sem("checked")
        starts_set = sem("starts_set")
        lined_in = [sem("lined_in_by_sp"), sem("lined_in_by_pool")]
        windows_in = sem("windows_in")
        lined_cast = sem("lined_cast")
        turned = sem("turned")
        key_step = sem("key_step")
        tests_summed = sem("tests_summed")
        flag_set = sem("flag_set")
        gather_begun = sem("gather_begun")
        idx_ready = sem("idx_ready")
        rel_ready = sem("rel_ready")
        onehot_ready = sem("onehot_ready")
        gathered = [sem(f"gathered{k}") for k in range(SLOTS)]
        summed = sem("summed")
        added = sem("added")
        cleared = sem("cleared")
        keys_ready = sem("keys_ready")
        rowhot_ready = sem("rowhot_ready")
        hot_ready = sem("hot_ready")
        hot_used = sem("hot_used")
        counts_out = sem("counts_out")
        ctab_out = [sem(f"ctab_out{k}") for k in range(2)]
        ctab_in = sem("ctab_in")
        last_counts_in = sem("last_counts_in")
        table_in = sem("table_in")
        applied_built = sem("applied_built")
        applied_loaded = sem("applied_loaded")
        squares_done = sem("squares_done")
        degree_done = sem("degree_done")
        rc_ready = sem("rc_ready")
        taken_step = [sem(f"taken_step{l}") for l in range(2)]
        linear_done = [sem(f"linear_done{l}") for l in range(2)]
        relu_done = sem("relu_done")
        split_step = sem("split_step")
        y_ready = sem("y_ready")
        norm_step = sem("norm_step")
        std_done = sem("std_done")
        stats_read = sem("stats_read")
        sp_held = sem("sp_held")
        h_out = [sem(f"h_out{k}") for k in range(BUFS)]
        y_out = [sem(f"y_out{k}") for k in range(BUFS)]
        res_in = [sem(f"res_in{k}") for k in range(BUFS)]

        block = ctx.enter_context(nc.Block())

        def tiles_of(g):
            return (TT, TP) if isinstance(g, int) and g == NG else (TILES, P)

        def gathers_before(layer, slot):
            n = 0
            for l in range(layer):
                n += sum(tiles_of(FIRST[l] + m)[0] for m in range(slot, GROUPS[l], SLOTS))
            return 16 * n

        def gathered_by(layer, i, step):
            slot = step % SLOTS
            if isinstance(i, int) and i * STEPS + step == GROUPS[layer] - 1:
                return gathers_before(layer + 1, slot)
            return i * (STEPS // SLOTS * TILES * 16) + ((step // SLOTS + 1) * TILES * 16 + gathers_before(layer, slot))

        def group_no(layer, i, step):
            return i * STEPS + (step + layer * (GROUPS[0] + BEYOND))

        def x_chunk(c):
            blocks = XCH if c < NXCH - 1 else 1
            return c * XCH, blocks, xin[:, c % XBUFS, 0:blocks, :]

        def load_lined(eng, b):
            start = eng.value_load(starts[0:1, b:b + 1], min_val=0, max_val=E - P * CTILES)
            row = b % TURN * CTILES
            eng.dma_start(lined[row:row + CTILES, :, b // TURN, :],
                          edge_list[:, bass.ds(start, P * CTILES)].rearrange("k (t e) -> t k e", e=P)
                          ).then_inc(lined_in[b >= LINED_BY_SP], 16)

        @block.sync
        def _(sp):
            def hold(sem, value):
                wait(sp, sem, value)
                if not isinstance(value, int):
                    sp.sem_inc(sp_held, 1)

            for k, run in ((0, run0), (1, run1), (EXACT, run256)):
                sp.dma_start(run, edge_list[1, k:k + P * SORTED_COLS].rearrange("(p j) -> p j", p=P)).then_inc(runs_in, 16)
            def load_x(c):
                first, blocks, place = x_chunk(c)
                if c >= XBUFS:
                    sp.wait_ge(rest_of_x, c - XBUFS + 1)
                if c < NXCH - 1:
                    rows = x[first * P:(first + blocks) * P, :].rearrange("(b p) c -> p b c", p=P)
                    sp.dma_start(place, rows).then_inc(x_in[c], 16)
                else:
                    sp.wait_ge(pad_set, 1)
                    sp.dma_start(place[0:LASTN, 0, :], x[first * P:N, :]).then_inc(x_in[c], 16)

            def store_x(c):
                first, blocks, _ = x_chunk(c)
                sp.wait_ge(parts_done, c + 1)
                sp.dma_start(xtab[first * P:(first + blocks) * P, :].rearrange("(b p) c -> p b c", p=P),
                             table[:, first:first + blocks, :]).then_inc(xtab_out, 16)

            load_x(0)
            sp.wait_ge(tail_set, 2)
            sp.dma_start(dst_all[:, 0:NG * TILES], dst_groups.rearrange("p g j -> p (g j)")).then_inc(edges_in, 16)
            sp.dma_start(dst_all[0:TP, NG * TILES:NG * TILES + TT], dst_tail).then_inc(edges_in, 16)
            load_x(1)
            sp.dma_start(idx_all[:, 0:NG * TILES], src_groups.rearrange("p g j -> p (g j)")).then_inc(edges_in, 16)
            sp.dma_start(idx_all[0:TP, NG * TILES:NG * TILES + TT], src_tail).then_inc(edges_in, 16)
            sp.dma_start(win, windows.rearrange("p (k n) -> p k n", k=2)).then_inc(windows_in, 16)
            sp.dma_start(unit[:], identity).then_inc(windows_in, 16)

            for c in range(2, XBUFS):
                load_x(c)
            sp.wait_ge(starts_set, 1)
            for b in range(LINED_BY_SP):
                load_lined(sp, b)
                if b in (3, 6):
                    load_x(XBUFS + b // 4)
                elif b in (5, 7):
                    store_x((b - 5) // 2)
            for c in range(XBUFS + 2, NXCH):
                load_x(c)
            for c in range(2, NXCH):
                store_x(c)
            sp.dma_start(wt[:, 0, :], w1t).then_inc(weights_in, 16)
            sp.dma_start(wt[:, 1, :], w2t).then_inc(weights_in, 16)
            sp.dma_start(bias[:, 0, :], b1).then_inc(weights_in, 16)
            sp.dma_start(bias[:, 1, :], b2).then_inc(weights_in, 16)

            def store_h(i, step):
                number, b, buf, _ = output(0, i, step)
                hold(split_step, number * 3 + 3)
                sp.dma_start(htab[bass.ds(b * P, P), :], hs[:, buf, :]).then_inc(h_out[buf], 16)

            def load_x_rows(i, step):
                number, b, buf, _ = output(1, i, step)
                hold(y_ready, number - 1)
                rows = LASTN if isinstance(b, int) and b == NB - 1 else P
                sp.dma_start(xres[0:rows, buf, :], x[bass.ds(b * P, rows), :]).then_inc(res_in[buf], 16)

            def store_y(i, step):
                number, b, buf, _ = output(1, i, step)
                hold(norm_step, number * 4 + 4)
                rows = LASTN if isinstance(b, int) and b == NB - 1 else P
                sp.dma_start(out[bass.ds(b * P, rows), :], yo[0:rows, buf, :]).then_inc(y_out[buf], 16)

            def all_h_stored(uses):
                for k in range(BUFS):
                    sp.wait_ge(h_out[k], 16 * uses[k])

            def all_y_stored(uses):
                for k in range(BUFS):
                    sp.wait_ge(y_out[k], 16 * uses[k])

            def fast():
                def store_counts(b, k):
                    first, end = STORED[k]
                    hold(counts_out, b * NPASS + end)
                    columns = slice(first * PASSW, end * PASSW)
                    sp.dma_start(ctab[bass.ds(b * P, P), columns], built[:, columns]).then_inc(ctab_out[k], 16)

                def round0(i):
                    first = isinstance(i, int) and i == 0
                    for step in OUTPUTS_FIRST[0] if first else OUTPUTS[0]:
                        if step in (4, 8):
                            store_counts(counted(0, i, step), 0)
                        store_h(i, step)
                        if step in (4, 8):
                            store_counts(counted(0, i, step), 1)

                round0(0)
                with sp.Fori(1, ROUNDS[0]) as i:
                    round0(i)
                for step in OUTPUTS_LEFT[0]:
                    store_h(ROUNDS[0], step)
                all_h_stored([buffer_uses(0, k) for k in range(BUFS)])
                sp.wait_ge(applied_built, COUNTED[0])
                sp.dma_start(table[:], htab.rearrange("(b p) c -> p b c", p=P)).then_inc(table_in, 16)

                def load_counts(b):
                    hold(applied_loaded, b)
                    for k in range(2):
                        sp.wait_ge(ctab_out[k], 16 * COUNTED[0])
                    sp.dma_start(loaded[:], ctab[bass.ds(b * P, P), :]).then_inc(ctab_in, 16)

                def round1(i):
                    first = isinstance(i, int) and i == 0
                    steps = OUTPUTS_FIRST[1] if first else OUTPUTS[1]
                    for k, step in enumerate(steps):
                        if k + 1 < len(steps):
                            load_x_rows(i, steps[k + 1])
                        else:
                            load_x_rows(i + 1, OUTPUTS[1][0])
                        if from_dram(1, i, step):
                            load_counts(output(1, i, step)[1] + 1)
                        store_y(i, step)

                load_counts(0)
                load_x_rows(0, OUTPUTS_FIRST[1][0])
                round1(0)
                with sp.Fori(1, ROUNDS[1]) as i:
                    round1(i)
                last = COUNTED[0] - 2
                sp.wait_ge(applied_built, COUNTED[1] + 1)
                sp.dma_start(built[:], ctab[last * P:(last + 1) * P, :]).then_inc(last_counts_in, 16)
                left = OUTPUTS_LEFT[1]
                for k, step in enumerate(left):
                    if k + 1 < len(left):
                        load_x_rows(ROUNDS[1], left[k + 1])
                    store_y(ROUNDS[1], step)
                all_y_stored([buffer_uses(1, k) for k in range(BUFS)])

            def general():
                uses = [NB // BUFS + (k < NB % BUFS) for k in range(BUFS)]

                def one_h(b, buf):
                    hold(split_step, b * 3 + 3)
                    sp.dma_start(htab[bass.ds(b * P, P), :], hs[:, buf, :]).then_inc(h_out[buf], 16)

                def one_y(b, buf):
                    rows = LASTN if isinstance(b, int) and b == NB - 1 else P
                    hold(y_ready, b)
                    sp.dma_start(xres[0:rows, buf, :], x[bass.ds(b * P, rows), :]).then_inc(res_in[buf], 16)
                    hold(norm_step, b * 4 + 4)
                    sp.dma_start(out[bass.ds(b * P, rows), :], yo[0:rows, buf, :]).then_inc(y_out[buf], 16)

                for one in (one_h, one_y):
                    for k in range(BUFS):
                        one(k, k)
                    with sp.Fori(1, NB // BUFS) as r:
                        for k in range(BUFS):
                            one(r * BUFS + k, k)
                    for b in range(NB // BUFS * BUFS, NB):
                        one(b, b % BUFS)
                all_h_stored(uses)
                all_y_stored(uses)

            sp.wait_ge(flag_set, 2)
            violated = sp.value_load(flag[0:1, 0:1], min_val=0, max_val=1 << 14)
            with sp.If(violated):
                general()
            with sp.Else():
                fast()

        @block.gpsimd
        def _(pool):
            nc.gpsimd.memset(idx_all[:, NG * TILES:], 0).then_inc(tail_set, 1)
            nc.gpsimd.memset(dst_all[:, NG * TILES:], N - 1).then_inc(tail_set, 1)
            nc.gpsimd.memset(eps[:], EPS).then_inc(consts_set, 1)
            nc.gpsimd.memset(onesf[:], 1.0).then_inc(consts_set, 1)
            nc.gpsimd.memset(ones[:], 1.0).then_inc(consts_set, 1)
            nc.gpsimd.memset(keys_all[:, :, KEYCOLS:], -1.0).then_inc(consts_set, 1)
            nc.gpsimd.iota(base_all.rearrange("p (g j) -> p g j", j=TILES), [[SHARE, EDGEW // TILES], [0, TILES]],
                           base=-MARGIN, channel_multiplier=0).then_inc(iota_set, 1)
            nc.gpsimd.iota(nodes[:], [[1, NB * SPAN]], base=0, channel_multiplier=0).then_inc(iota_set, 1)
            pool.wait_ge(starts_set, 1)
            for b in range(LINED_BY_SP, COUNTED[1]):
                load_lined(pool, b)
            pool.wait_ge(rest_of_x, NXCH - XBUFS)
            nc.gpsimd.memset(x_chunk(NXCH - 1)[2], 0.0).then_inc(pad_set, 1)

            def gather(layer, g, slot, groups_done, h_uses):
                tiles, parts = tiles_of(g)
                if layer == 0:
                    pool.wait_ge(xtab_out, 16 * NXCH)
                else:
                    for k in range(BUFS):
                        pool.wait_ge(h_out[k], 16 * h_uses[k])
                pool.wait_ge(idx_ready, groups_done + 1)
                pool.sem_inc(gather_begun, 1)
                for j in range(tiles):
                    nc.gpsimd.indirect_dma_start(
                        out=msg[0:parts, slot, j, :], out_offset=None, in_=tables[layer],
                        in_offset=bass.IndirectOffsetOnAxis(ap=idx[0:parts, slot, j:j + 1], axis=0),
                    ).then_inc(gathered[slot], 16)

            def fast():
                uses = [buffer_uses(0, k) for k in range(BUFS)]
                for layer in range(2):
                    with pool.Fori(0, ROUNDS[layer]) as i:
                        for step in range(STEPS):
                            gather(layer, None, step % SLOTS, group_no(layer, i, step), uses)
                    for m in range(ROUNDS[layer] * STEPS, GROUPS[layer]):
                        gather(layer, FIRST[layer] + m, m % SLOTS, group_no(layer, 0, m), uses)

            def general():
                uses = [NB // BUFS + (k < NB % BUFS) for k in range(BUFS)]
                for layer in range(2):
                    with pool.Fori(0, NG) as g:
                        gather(layer, g, 0, g + layer * G, uses)
                    gather(layer, NG, 0, NG + layer * G, uses)

            pool.wait_ge(flag_set, 2)
            violated = pool.value_load(flag[0:1, 0:1], min_val=0, max_val=1 << 14)
            with pool.If(violated):
                general()
            with pool.Else():
                fast()

        @block.tensor
        def _(pe):
            pe.wait_ge(consts_set, 4)
            pe.wait_ge(checked, 6)
            pe.matmul(ps_lin[:, 1:1 + COUNTED[1]], onesf[:], tests[:, 1:], start=True, stop=True
                      ).then_inc(tests_summed, 1)
            pe.wait_ge(lined_cast, 2)
            pe.wait_ge(windows_in, 32)
            for k, bank in enumerate((ps_count[:, 0, :], ps_apply[:])):
                for g in range(NTURN):
                    tiles = min(TURN, COUNTED[1] - g * TURN) * CTILES
                    at = g * TURN * CTILES
                    mm = pe.matmul(bank[:, at:at + tiles], lined_f32[0:tiles, k, g, :], unit[0:tiles, 0:tiles],
                                   start=True, stop=True)
            mm.then_inc(turned, 1)
            pe.wait_ge(checked, 15)
            pe.matmul(ps_lin[:, 0:1], onesf[:], tests[:, 0:1], start=True, stop=True).then_inc(tests_summed, 1)
            pe.wait_ge(weights_in, 64)

            def sum_rows(sums, counts, rows, hot, tiles, parts, groups=1):
                for j in range(tiles):
                    for s in range(PARTS):
                        mm = pe.matmul(sums, rows[0:parts, j, s * C:(s + 1) * C], hot[0:parts, j, :],
                                       start=(j == 0 and s == 0), stop=(j == tiles - 1 and s == PARTS - 1))
                if counts is not None:
                    for j in range(tiles):
                        mm = pe.matmul(counts, ones[0:parts, :], hot[0:parts, j, :],
                                       start=(j == 0), stop=(j == tiles - 1))
                mm.then_inc(summed, groups)

            def linear(layer, number):
                pe.wait_ge(taken_step[layer], number * 2 + 2)
                if layer == 0:
                    wait(pe, relu_done, number * 2)
                else:
                    wait(pe, y_ready, number)
                pe.matmul(ps_lin[:, CAT:CAT + 1], taken[0:1, 1, :], onesf[0:1, 0:1], start=True, stop=True)
                pe.matmul(ps_lin[:, 0:C], taken[:, 0, :], wt[:, layer, :], start=True, stop=False)
                pe.matmul(ps_lin[:, 0:C], taken[0:1, 1, :], bias[:, layer, :], start=False, stop=True
                          ).then_inc(linear_done[layer], 1)

            def fast():
                for layer in range(2):
                    def group(i, step):
                        n = group_no(layer, i, step)
                        last = isinstance(i, int) and i * STEPS + step == GROUPS[layer] - 1
                        tiles, parts = tiles_of(NG) if last else (TILES, P)
                        bank = ps_group[step % 2]
                        pe.wait_ge(onehot_ready, n + 1)
                        pe.wait_ge(gathered[step % SLOTS], gathered_by(layer, i, step))
                        wait(pe, added, n - 1)
                        sum_rows(bank[:, 0:W], bank[:, CAT:CAT + W] if layer == 0 else None,
                                 msg[:, step % SLOTS], onehot[:, step % SLOTS], tiles, parts,
                                 groups=1 + BEYOND if last else 1)

                    def count_pass(d, p):
                        half = 2 * (p % 2)
                        wait(pe, counts_out, d * NPASS + (p - 1 if p else 0))
                        if p == 0:
                            pe.wait_ge(rowhot_ready, d + 1)
                        banks = [ps_count[:, half + k, 0:blocks * P] for k, (_, blocks) in enumerate(HALVES)]
                        for c in range(CHUNKS):
                            q = p * CHUNKS + c
                            pe.wait_ge(hot_ready, d * NHOT + (q + 1))
                            for t, (tile, covered) in enumerate(ORDER[c * HOT_TILES:(c + 1) * HOT_TILES]):
                                first = tile_first(tile, TILE_SHARE)
                                new = min(max(covered - first, 0), SPAN)
                                parts = [part for part in ((0, new), (new, SPAN)) if part[0] < part[1]]
                                for (b, blocks), bank in zip(HALVES, banks):
                                    nodes_of = bank.rearrange("p (b n) -> p b n", n=P)
                                    hot = colhot[:, q % HOT_BUFS, t, b * SPAN:(b + blocks) * SPAN].rearrange(
                                        "p (b n) -> p b n", n=SPAN)
                                    for at, end in parts:
                                        mm = pe.matmul(nodes_of[:, :, first + at:first + end], rowhot[:, tile, :],
                                                       hot[:, :, at:end], start=(c == 0 and t == 0),
                                                       stop=(c * HOT_TILES + t == CTILES - 1))
                            mm.then_inc(hot_used, 1)

                    def apply(counts, blocks, applied):
                        for q in blocks:
                            columns = counts[:, q * P:(q + 1) * P]
                            for s in range(PARTS):
                                mm = pe.matmul(ps_apply[:, 0:C], table[:, q, s * C:(s + 1) * C], columns,
                                               start=(q == 0 and s == 0),
                                               stop=(layer == 1 and q == NB - 1 and s == PARTS - 1))
                            if layer == 0:
                                mm = pe.matmul(ps_apply[:, CAT:CAT + P], ones[:], columns,
                                               start=False, stop=(q == NB - 1))
                        if NB - 1 in blocks:
                            mm.then_inc(applied, 1)

                    def apply_loaded(i, step):
                        b = output(1, i, step)[1]
                        if isinstance(i, int) and b == 0:
                            pe.wait_ge(table_in, 16)
                        pe.wait_ge(ctab_in, b * 16 + 16)
                        apply(loaded, range(NB), applied_loaded)

                    def apply_pass(d, p):
                        if layer == 0:
                            pe.wait_ge(parts_done, NXCH)
                        pe.wait_ge(counts_out, d * NPASS + (p + 1))
                        apply(built, range(p * PASS_BLOCKS, (p + 1) * PASS_BLOCKS), applied_built)

                    def one_round(i):
                        first = isinstance(i, int) and i == 0
                        outputs = (OUTPUTS_FIRST if first else OUTPUTS)[layer]
                        for step in range(STEPS):
                            d = counted(layer, i, step)
                            group(i, step)
                            passes = PASSES[layer][step] if counts_at(layer, i) else ()
                            for p in passes:
                                count_pass(d, p)
                            if step in outputs and step % 2:
                                linear(layer, output(layer, i, step)[0])
                            if counts_at(layer, i) or step == STEPS - 1:
                                for p in APPLIED[layer][step]:
                                    apply_pass(d, p)
                            if step + 1 in outputs and from_dram(layer, i, step + 1):
                                apply_loaded(i, step + 1)
                            if step in outputs and step % 2 == 0:
                                linear(layer, output(layer, i, step)[0])

                    if layer == 1:
                        pe.wait_ge(relu_done, 2 * NB)
                    one_round(0)
                    with pe.Fori(1, ROUNDS[layer]) as i:
                        one_round(i)
                    i, last = ROUNDS[layer], LEFT[layer] - 1
                    for step in OUTPUTS_LEFT[layer][:BEFORE_LAST[layer]]:
                        if step < last:
                            group(i, step)
                        linear(layer, output(layer, i, step)[0])
                        if layer == 1 and step == 1:
                            apply_loaded(i, 3)
                        if layer == 1 and step == 3:
                            pe.wait_ge(last_counts_in, 16)
                            apply(built, range(NB), applied_loaded)
                    group(i, last)
                    for step in OUTPUTS_LEFT[layer][BEFORE_LAST[layer]:]:
                        linear(layer, output(layer, i, step)[0])

            def general():
                for layer in range(2):
                    def chunk(n, c, tiles, parts, landed):
                        q = n * NCHUNK + c
                        pe.wait_ge(gathered[0], landed)
                        pe.wait_ge(onehot_ready, q + 1)
                        sum_rows(ps_group[0][:, 0:CHUNK], ps_group[1][:, 0:CHUNK], msg[:, 0], wide_onehot,
                                 tiles, parts)
                    with pe.Fori(0, NG) as g:
                        landed = (g + 1) * (16 * TILES) + layer * 16 * (NG * TILES + TT)
                        with pe.Fori(0, NCHUNK) as c:
                            chunk(g + layer * G, c, TILES, P, landed)
                    with pe.Fori(0, NCHUNK) as c:
                        chunk(NG + layer * G, c, TT, TP, (layer + 1) * 16 * (NG * TILES + TT))
                    if layer == 1:
                        pe.wait_ge(relu_done, 2 * NB)
                    linear(layer, 0)
                    with pe.Fori(1, NB) as b:
                        linear(layer, b)

            pe.wait_ge(flag_set, 2)
            violated = pe.value_load(flag[0:1, 0:1], min_val=0, max_val=1 << 14)
            with pe.If(violated):
                general()
            with pe.Else():
                fast()

        @block.scalar
        def _(act):
            for c in range(NXCH + 1):
                if c < NXCH:
                    first, blocks, place = x_chunk(c)
                    act.wait_ge(x_in[c], 16)
                    nc.scalar.activation(table[:, first:first + blocks, 0:C], place, ACT.Copy).then_inc(first_part, 1)
                if c > 0:
                    first, blocks, _ = x_chunk(c - 1)
                    act.wait_ge(rest_of_x, c)
                    nc.scalar.activation(table[:, first:first + blocks, C:2 * C], xrest[:, (c - 1) % 2, 0:blocks, :],
                                         ACT.Copy).then_inc(second_part, 1)

            def take(layer, number, b, product=False):
                at = bass.ds(b * P + MARGIN, P)
                wait(act, linear_done[layer], number)
                if not product:
                    nc.scalar.activation(taken[:], acc[:, :, at], ACT.Copy).then_inc(taken_step[layer], 2)
                    return
                found = ps_apply[:].rearrange("p (k n) -> p k n", k=2)[:, :, 0:P]
                if layer == 0:
                    nc.scalar.activation(taken[:], found, ACT.Copy).then_inc(taken_step[layer], 1)
                    nc.scalar.activation(cnt[:, at], found[:, 1, :], ACT.Copy).then_inc(taken_step[layer], 1)
                else:
                    nc.scalar.activation(taken[:, 0, :], found[:, 0, :], ACT.Copy).then_inc(taken_step[layer], 1)
                    nc.scalar.activation(taken[:, 1, :], cnt[:, at], ACT.Copy).then_inc(taken_step[layer], 1)

            def relu(number, buf, uses):
                act.wait_ge(rc_ready, number + 1)
                wait(act, split_step, number * 3)
                wait(act, h_out[buf], uses * 16)
                nc.scalar.activation(h32[:], ps_lin[:, 0:C], ACT.Relu, scale=rc[:, 0:1]).then_inc(relu_done, 1)
                nc.scalar.activation(hs[:, buf, 0:C], ps_lin[:, 0:C], ACT.Relu, scale=rc[:, 0:1]).then_inc(relu_done, 1)

            def deviation(number):
                act.wait_ge(norm_step, number * 4 + 2)
                nc.scalar.activation(std[:], mv[:, 1:2], ACT.Sqrt, bias=eps[:, 0:1]).then_inc(std_done, 1)

            def fast():
                for layer in range(2):
                    def keep_counts(d, p):
                        half = 2 * (p % 2)
                        if p == 0:
                            wait(act, applied_built, d + layer)
                        if layer == 0 and p in (STORED[0][0], STORED[1][0]):
                            wait(act, ctab_out[p // STORED[1][0]], d * 16)
                        act.wait_ge(hot_used, d * NHOT + (p + 1) * CHUNKS)
                        found = ps_count[:, half:half + 2, :].rearrange("p k n -> p (k n)")[:, 0:PASSW]
                        nc.scalar.activation(built[:, p * PASSW:(p + 1) * PASSW], found, ACT.Copy
                                             ).then_inc(counts_out, 1)

                    def one_hots(i, step):
                        n = group_no(layer, i, step)
                        hot = onehot[:, step % SLOTS]
                        act.wait_ge(idx_ready, n + 1)
                        for j in range(TILES):
                            op = nc.scalar.activation(hot[:, j, :], nodes[:, 0:W], ACT.Square,
                                                      bias=rel[:, step % SLOTS, j:j + 1])
                        op.then_inc(squares_done, 1)
                        act.wait_ge(squares_done, n + 1)
                        nc.scalar.activation(hot, hot, ACT.Relu, bias=onesf[:, 0:1], scale=-1.0).then_inc(onehot_ready, 1)

                    def begin(i, step, groups):
                        number, b, _, _ = output(layer, i, step)
                        if step % 2 == 0:
                            act.wait_ge(added, group_no(layer, i, groups))
                        elif from_dram(layer, i, step):
                            act.wait_ge(applied_loaded, b + 1)
                        else:
                            act.wait_ge(applied_built, b + (1 + layer))
                        take(layer, number, b, product=step % 2 == 1)

                    def end(i, step):
                        if layer == 0:
                            number, _, buf, uses = output(0, i, step)
                            relu(number, buf, uses)
                        else:
                            deviation(output(1, i, step)[0])

                    def one_round(i):
                        first = isinstance(i, int) and i == 0
                        outputs = (OUTPUTS_FIRST if first else OUTPUTS)[layer]
                        for step in range(STEPS):
                            if step - 1 in outputs:
                                end(i, step - 1)
                            if step in outputs:
                                begin(i, step, step)
                            one_hots(i, step + LEAD)
                            for p in PASSES[layer][step] if counts_at(layer, i) else ():
                                keep_counts(counted(layer, i, step), p)

                    if layer == 1:
                        act.wait_ge(relu_done, 2 * NB)
                    for step in range(LEAD):
                        one_hots(0, step)
                    one_round(0)
                    with act.Fori(1, ROUNDS[layer]) as i:
                        one_round(i)
                    i = ROUNDS[layer]
                    for step in OUTPUTS_LEFT[layer]:
                        begin(i, step, min(step, LEFT[layer]))
                        if step + LEAD < LEFT[layer]:
                            one_hots(i, step + LEAD)
                        end(i, step)

            def general():
                act.wait_ge(added, G * NCHUNK)
                for k in range(BUFS):
                    take(0, k, k)
                    relu(k, k, 0)
                with act.Fori(1, NB // BUFS) as r:
                    for k in range(BUFS):
                        take(0, r * BUFS + k, r * BUFS + k)
                        relu(r * BUFS + k, k, r)
                for b in range(NB // BUFS * BUFS, NB):
                    take(0, b, b)
                    relu(b, b % BUFS, NB // BUFS)
                act.wait_ge(added, 2 * G * NCHUNK)
                take(1, 0, 0)
                deviation(0)
                with act.Fori(1, NB) as b:
                    take(1, b, b)
                    deviation(b)

            act.wait_ge(flag_set, 2)
            violated = act.value_load(flag[0:1, 0:1], min_val=0, max_val=1 << 14)
            with act.If(violated):
                general()
            with act.Else():
                fast()

        @block.vector
        def _(dve):
            dve.wait_ge(runs_in, 48)
            nc.vector.tensor_tensor(order[:], run0, run1, ALU.is_gt).then_inc(checked, 1)
            dve.wait_ge(checked, 1)
            nc.vector.tensor_reduce(lim[:, 4:5], order[:], AX.X, ALU.max).then_inc(checked, 1)
            dve.wait_ge(checked, 2)
            nc.vector.tensor_tensor(order[:], run0, run256, ALU.is_equal).then_inc(checked, 1)
            dve.wait_ge(checked, 3)
            nc.vector.tensor_reduce(lim[:, 5:6], order[:], AX.X, ALU.max).then_inc(checked, 1)
            dve.wait_ge(checked, 4)
            nc.vector.tensor_copy(short, run0).then_inc(checked, 1)
            dve.wait_ge(checked, 5)
            for b in range(1, COUNTED[1] + 1):
                last = nc.vector.tensor_scalar(before[:, b - 1, :], short, float(b * P), None, ALU.is_lt, ALU.add,
                                               accum_out=tests[:, b:b + 1])
            last.then_inc(checked, 1)
            nc.vector.memset(sums[:, 0:1], 0.0).then_inc(cleared, 1)
            dve.wait_ge(tests_summed, 1)
            dve.wait_ge(cleared, 1)
            nc.vector.tensor_copy(sums[:, 1:], ps_lin[:, 1:1 + COUNTED[1]]).then_inc(checked, 1)
            dve.wait_ge(checked, 7)
            nc.vector.tensor_copy(starts[:], sums[:]).then_inc(starts_set, 1)
            nc.vector.tensor_tensor(span[:], sums[:, 1:1 + COUNTED[1]], sums[:, 0:COUNTED[1]], ALU.subtract
                                    ).then_inc(checked, 1)
            dve.wait_ge(checked, 8)
            nc.vector.tensor_reduce(lim[:, 8:9], span[:], AX.X, ALU.max).then_inc(checked, 1)
            dve.wait_ge(checked, 9)
            nc.vector.tensor_scalar(lim[:, 6:7], lim[:, 8:9], P * CTILES + 0.5, None, ALU.is_gt).then_inc(checked, 1)
            dve.wait_ge(edges_in, 64)
            dve.wait_ge(iota_set, 2)
            nc.vector.tensor_tensor(rel_all, base_all, dst_all[:], ALU.subtract).then_inc(checked, 1)
            dve.wait_ge(checked, 11)
            nc.vector.tensor_reduce(lim[:, 0:1], rel_all[:, 0:G * TILES], AX.X, ALU.min).then_inc(checked, 1)
            nc.vector.tensor_reduce(lim[:, 1:2], rel_all[:, 0:G * TILES], AX.X, ALU.max).then_inc(checked, 1)

            def first_rest(c):
                first, blocks, place = x_chunk(c)
                rest = xrest[:, c % 2, 0:blocks, :]
                if c >= 2:
                    dve.wait_ge(parts_done, c - 1)
                dve.wait_ge(first_part, c + 1)
                nc.vector.tensor_tensor(rest, place, table[:, first:first + blocks, 0:C], ALU.subtract
                                        ).then_inc(rest_of_x, 1)

            def third_part(c):
                first, blocks, _ = x_chunk(c)
                rest = xrest[:, c % 2, 0:blocks, :]
                dve.wait_ge(rest_of_x, c + 1)
                dve.wait_ge(second_part, c + 1)
                nc.vector.tensor_tensor(table[:, first:first + blocks, 2 * C:3 * C], rest,
                                        table[:, first:first + blocks, C:2 * C], ALU.subtract
                                        ).then_inc(parts_done, 1)

            def cast_lined():
                dve.wait_ge(lined_in[0], 16 * LINED_BY_SP)
                dve.wait_ge(lined_in[1], 16 * (COUNTED[1] - LINED_BY_SP))
                full = COUNTED[1] // TURN
                rest = (COUNTED[1] - full * TURN) * CTILES
                nc.vector.tensor_copy(lined_f32[0:TURN * CTILES, :, 0:full, :], lined[0:TURN * CTILES, :, 0:full, :]
                                      ).then_inc(lined_cast, 1)
                nc.vector.tensor_copy(lined_f32[0:rest, :, full, :], lined[0:rest, :, full, :]).then_inc(lined_cast, 1)

            first_rest(0)
            for c in range(NXCH):
                if c == CAST_AT:
                    cast_lined()
                if c + 1 < NXCH:
                    first_rest(c + 1)
                third_part(c)
            dve.wait_ge(turned, 1)
            dve.wait_ge(windows_in, 32)
            src_of, dst_of = ps_count[:, 0, 0:KEYCOLS], ps_apply[:, 0:KEYCOLS]
            nc.vector.tensor_copy(source, src_of).then_inc(key_step, 1)
            nc.vector.tensor_tensor(from_window, dst_of, win[:, 0, :], ALU.subtract).then_inc(key_step, 1)
            nc.vector.tensor_tensor(in_block, dst_of, win[:, 1, :], ALU.is_lt).then_inc(key_step, 1)
            dve.wait_ge(key_step, 3)
            nc.vector.tensor_scalar(low, source, P - 1, None, ALU.bitwise_and).then_inc(key_step, 1)
            nc.vector.tensor_scalar(not_before, from_window, 0.0, None, ALU.is_ge).then_inc(key_step, 1)
            dve.wait_ge(key_step, 5)
            nc.vector.tensor_copy(keys_all[:, 0, 0:KEYCOLS], low).then_inc(key_step, 1)
            nc.vector.scalar_tensor_tensor(out=inside, in0=from_window, scalar=float(SPAN), in1=not_before,
                                           op0=ALU.is_lt, op1=ALU.mult).then_inc(key_step, 1)
            dve.wait_ge(key_step, 7)
            nc.vector.tensor_tensor(from_block, src_of, keys_all[:, 0, 0:KEYCOLS], ALU.subtract).then_inc(key_step, 1)
            nc.vector.tensor_tensor(outside, in_block, inside, ALU.subtract).then_inc(key_step, 1)
            dve.wait_ge(key_step, 9)
            nc.vector.scalar_tensor_tensor(out=column, in0=from_block, scalar=SPAN / P, in1=from_window,
                                           op0=ALU.mult, op1=ALU.add).then_inc(key_step, 1)
            nc.vector.tensor_reduce(lim[:, 7:8], outside, AX.X, ALU.max).then_inc(key_step, 1)
            dve.wait_ge(key_step, 11)
            nc.vector.scalar_tensor_tensor(out=column1, in0=column, scalar=1.0, in1=inside,
                                           op0=ALU.add, op1=ALU.mult).then_inc(key_step, 1)
            dve.wait_ge(key_step, 12)
            nc.vector.tensor_scalar(keys_all[:, 1, 0:KEYCOLS], column1, -1.0, None, ALU.add).then_inc(key_step, 1)
            dve.wait_ge(checked, 13)
            nc.vector.tensor_scalar(lim[:, 2:3], lim[:, 0:1], 0.5 - W, None, ALU.is_lt).then_inc(checked, 1)
            nc.vector.tensor_scalar(lim[:, 3:4], lim[:, 1:2], 0.5, None, ALU.is_gt).then_inc(key_step, 1)
            dve.wait_ge(checked, 14)
            dve.wait_ge(key_step, 14)
            nc.vector.tensor_reduce(tests[:, 0:1], lim[:, 2:8], AX.X, ALU.max).then_inc(checked, 1)
            dve.wait_ge(tests_summed, 2)
            nc.vector.tensor_copy(flag[:], ps_lin[:, 0:1]).then_inc(flag_set, 2)

            def degrees(layer, number):
                n = number + layer * NB
                dve.wait_ge(linear_done[layer], number + 1)
                nc.vector.tensor_scalar(degree[:], ps_lin[:, CAT:CAT + 1], 1.0, None, ALU.max).then_inc(degree_done, 1)
                dve.wait_ge(degree_done, n + 1)
                nc.vector.reciprocal(rc[:, layer:layer + 1], degree[:]).then_inc(rc_ready, 1)

            def split_h(number, buf):
                n = number * 3
                dve.wait_ge(relu_done, number * 2 + 2)
                nc.vector.tensor_tensor(hr[:], h32[:], hs[:, buf, 0:C], ALU.subtract).then_inc(split_step, 1)
                dve.wait_ge(split_step, n + 1)
                nc.vector.tensor_copy(hs[:, buf, C:2 * C], hr[:]).then_inc(split_step, 1)
                dve.wait_ge(split_step, n + 2)
                nc.vector.tensor_tensor(hs[:, buf, 2 * C:3 * C], hr[:], hs[:, buf, C:2 * C],
                                        ALU.subtract).then_inc(split_step, 1)

            def residual(number, b, buf, uses):
                n = number * 4
                rows = LASTN if isinstance(b, int) and b == NB - 1 else P
                dve.wait_ge(rc_ready, number + (NB + 1))
                wait(dve, norm_step, n)
                dve.wait_ge(res_in[buf], uses * 16 + 16)
                nc.vector.scalar_tensor_tensor(out=y[0:rows, :], in0=ps_lin[0:rows, 0:C], scalar=rc[0:rows, 1:2],
                                               in1=xres[0:rows, buf, :], op0=ALU.mult, op1=ALU.add
                                               ).then_inc(y_ready, 1)
                dve.wait_ge(y_ready, number + 1)
                nc.vector.bn_stats(stats[:], y[:]).then_inc(norm_step, 1)
                dve.wait_ge(norm_step, n + 1)
                dve.sem_inc(stats_read, 1)
                nc.vector.bn_aggr(mv[:], stats[:]).then_inc(norm_step, 1)

            def norm(number, buf, uses):
                n = number * 4
                dve.wait_ge(std_done, number + 1)
                nc.vector.reciprocal(rstd[:], std[:]).then_inc(norm_step, 1)
                dve.wait_ge(norm_step, n + 3)
                wait(dve, y_out[buf], uses * 16)
                nc.vector.tensor_scalar(yo[:, buf, :], y[:], mv[:, 0:1], rstd[:, 0:1],
                                        ALU.subtract, ALU.mult).then_inc(norm_step, 1)

            def fast():
                def block_keys(d):
                    wait(dve, hot_ready, d * NHOT)
                    nc.vector.tensor_copy(keys[:], keys_all[:, :, bass.ds(d * CTILES, CTILES)]).then_inc(keys_ready, 1)

                def row_rows(d):
                    wait(dve, hot_used, d * NHOT)
                    for t in range(CTILES):
                        op = nc.vector.tensor_scalar(rowhot[:, t, :], nodes[:, 0:P], keys[:, 0, t:t + 1], None,
                                                     ALU.is_equal)
                    op.then_inc(rowhot_ready, 1)

                def hot_rows(d, p):
                    if p == 0:
                        dve.wait_ge(keys_ready, d + 1)
                    for c in range(CHUNKS):
                        q = p * CHUNKS + c
                        wait(dve, hot_used, d * NHOT + (q + 1 - HOT_BUFS))
                        for t in range(HOT_TILES):
                            tile, _ = ORDER[c * HOT_TILES + t]
                            op = nc.vector.tensor_scalar(colhot[:, q % HOT_BUFS, t, :], nodes[:, p * HOTW:(p + 1) * HOTW],
                                                         keys[:, 1, tile:tile + 1], None, ALU.is_equal)
                        op.then_inc(hot_ready, 1)

                for layer in range(2):
                    def prepare(i, step):
                        n = group_no(layer, i, step)
                        slot = step % SLOTS
                        wait(dve, summed, n - (SLOTS - 1))
                        at = bass.ds((i * STEPS + (step + FIRST[layer])) * (2 * TILES), 2 * TILES)
                        nc.vector.tensor_copy(edges[:, slot].bitcast(I16), edges_all[:].bitcast(I16)[:, :, at]
                                              ).then_inc(idx_ready, 1)

                    def evacuate(i, step):
                        n = group_no(layer, i, step)
                        kinds = 2 if layer == 0 else 1
                        bank = ps_group[step % 2][:].rearrange("p (k n) -> p k n", k=2)[:, 0:kinds, :]
                        dve.wait_ge(summed, n + 1)
                        wait(dve, added, n)
                        at = (i * STEPS + (step + FIRST[layer])) * SHARE
                        old, new = bass.ds(at, OLD), bass.ds(at + OLD, SHARE)
                        nc.vector.tensor_tensor(acc[:, 0:kinds, old], acc[:, 0:kinds, old], bank[:, :, 0:OLD], ALU.add)
                        last = isinstance(i, int) and i * STEPS + step == GROUPS[layer] - 1
                        nc.vector.tensor_copy(acc[:, 0:kinds, new], bank[:, :, OLD:W]
                                              ).then_inc(added, 1 + BEYOND if last else 1)

                    def begin(i, step):
                        number, b, buf, uses = output(layer, i, step)
                        degrees(layer, number)
                        if layer == 1:
                            residual(number, b, buf, uses)

                    def end(i, step):
                        number, b, buf, uses = output(layer, i, step)
                        if layer == 0:
                            split_h(number, buf)
                        else:
                            norm(number, buf, uses)

                    def one_round(i, last_counts=False):
                        first = isinstance(i, int) and i == 0
                        outputs = (OUTPUTS_FIRST if first else OUTPUTS)[layer]
                        for step in range(STEPS):
                            prepare(i, step + LEAD)
                            if step - 2 in outputs:
                                end(i, step - 2)
                            if step - 1 in outputs:
                                begin(i, step - 1)
                            evacuate(i, step)
                            if step == STEPS - 1:
                                end(i, step - 1)
                            d = counted(layer, i, step)
                            if counts_at(layer, i):
                                for p in PASSES[layer][step]:
                                    if p + 2 < NPASS:
                                        hot_rows(d, p + 2)
                                if last_counts and step >= 5:
                                    continue
                                if step % 5 == 3:
                                    block_keys(d + 1)
                                    hot_rows(d + 1, 0)
                                if step % 5 == 4:
                                    row_rows(d + 1)
                                    hot_rows(d + 1, 1)

                    first_old = slice(FIRST[layer] * SHARE, FIRST[layer] * SHARE + OLD)
                    if layer == 0:
                        nc.vector.memset(cnt[:, first_old], 0.0).then_inc(cleared, 1)
                    nc.vector.memset(agg[:, first_old], 0.0).then_inc(cleared, 1)
                    dve.wait_ge(cleared, 3 + layer)
                    if layer == 1:
                        dve.wait_ge(onehot_ready, GROUPS[0] + BEYOND)
                    for step in range(LEAD):
                        prepare(0, step)
                    if layer == 0:
                        dve.wait_ge(consts_set, 4)
                    b = layer * COUNTED[0]
                    block_keys(b)
                    hot_rows(b, 0)
                    row_rows(b)
                    hot_rows(b, 1)
                    one_round(0)
                    with dve.Fori(1, ROUNDS[layer] - 1) as i:
                        one_round(i)
                    one_round(ROUNDS[layer] - 1, last_counts=True)
                    i, last = ROUNDS[layer], LEFT[layer] - 1
                    for step in OUTPUTS_LEFT[layer][:BEFORE_LAST[layer]]:
                        if step + LEAD <= last:
                            prepare(i, step + LEAD)
                        begin(i, step)
                        end(i, step)
                        if step < last:
                            evacuate(i, step)
                    evacuate(i, last)
                    for step in OUTPUTS_LEFT[layer][BEFORE_LAST[layer]:]:
                        begin(i, step)
                        end(i, step)

            def general():
                for layer in range(2):
                    def all_chunks(column, n):
                        at = bass.ds(column, TILES)
                        nc.vector.tensor_copy(idx[:, 0, :], idx_all[:, at]).then_inc(idx_ready, 1)
                        wait(dve, rel_ready, n * (NCHUNK + 1))
                        nc.vector.tensor_copy(rel[:, 0, :], dst_all[:, at]).then_inc(rel_ready, 1)
                        with dve.Fori(0, NCHUNK) as c:
                            q = n * NCHUNK + c
                            dve.wait_ge(rel_ready, n * (NCHUNK + 1) + c + 1)
                            for j in range(TILES):
                                op = nc.vector.tensor_scalar(wide_onehot[:, j, :], nodes[:, 0:CHUNK],
                                                             rel[:, 0, j:j + 1], None, ALU.is_equal)
                            op.then_inc(onehot_ready, 1)
                            dve.wait_ge(summed, q + 1)
                            at = bass.ds(c * CHUNK + MARGIN, CHUNK)
                            if layer == 0:
                                nc.vector.tensor_tensor(cnt[:, at], cnt[:, at], ps_group[1][:, 0:CHUNK], ALU.add)
                            nc.vector.tensor_tensor(agg[:, at], agg[:, at], ps_group[0][:, 0:CHUNK], ALU.add
                                                    ).then_inc(added, 1)
                            dve.wait_ge(added, q + 1)
                            nc.vector.tensor_scalar(rel[:, 0, :], rel[:, 0, :], float(-CHUNK), None, ALU.add
                                                    ).then_inc(rel_ready, 1)

                    if layer == 0:
                        nc.vector.memset(cnt, 0.0).then_inc(cleared, 1)
                    nc.vector.memset(agg, 0.0).then_inc(cleared, 1)
                    dve.wait_ge(cleared, 3 + layer)
                    all_chunks(0, layer * G)
                    with dve.Fori(1, NG) as g:
                        all_chunks(g * TILES, g + layer * G)
                    all_chunks(NG * TILES, NG + layer * G)

                    def one(b, buf, uses):
                        degrees(layer, b)
                        if layer == 0:
                            split_h(b, buf)
                        else:
                            residual(b, b, buf, uses)
                            norm(b, buf, uses)
                    for k in range(BUFS):
                        one(k, k, 0)
                    with dve.Fori(1, NB // BUFS) as r:
                        for k in range(BUFS):
                            one(r * BUFS + k, k, r)
                    for b in range(NB // BUFS * BUFS, NB):
                        one(b, b % BUFS, NB // BUFS)

            dve.wait_ge(flag_set, 2)
            violated = dve.value_load(flag[0:1, 0:1], min_val=0, max_val=1 << 14)
            with dve.If(violated):
                general()
            with dve.Else():
                fast()


def kernel(x, src, dst, L0_gnn_W1, L0_gnn_b1, L0_gnn_W2, L0_gnn_b2):
    import numpy as _np
    import concourse.bacc as _bacc
    from concourse import mybir as _mybir
    from concourse.bass_utils import run_bass_kernel_spmd as _run

    src, dst = _np.asarray(src), _np.asarray(dst)
    full = src.shape[0] // GROUP_EDGES
    tiles, parts = split_of_tail(src.shape[0] - full * GROUP_EDGES)

    def groups(e):
        return _np.ascontiguousarray(e[:full * GROUP_EDGES].reshape(full, P, TILES).transpose(1, 0, 2))

    def tail(e):
        return _np.ascontiguousarray(e[full * GROUP_EDGES:].reshape(parts, tiles))

    arrays = {
        "x": _np.ascontiguousarray(x),
        "edge_list": _np.stack([src, dst]),
        "src_groups": groups(src), "dst_groups": groups(dst),
        "src_tail": tail(src), "dst_tail": tail(dst),
        "w1t": _np.ascontiguousarray(_np.asarray(L0_gnn_W1).T), "b1": _np.asarray(L0_gnn_b1).reshape(1, -1),
        "w2t": _np.ascontiguousarray(_np.asarray(L0_gnn_W2).T), "b2": _np.asarray(L0_gnn_b2).reshape(1, -1),
    }
    blocks = _np.repeat(_np.arange(COUNTED[1]) * P, CTILES)
    firsts = _np.tile([tile_first(t, x.shape[0] * P // src.shape[0]) for t in range(CTILES)], COUNTED[1])
    windows = _np.concatenate([blocks + firsts, blocks + P]).astype(_np.float32)
    arrays["windows"] = _np.ascontiguousarray(_np.broadcast_to(windows, (P, windows.size)))
    arrays["identity"] = _np.eye(P, dtype=_np.float32)
    nc = _bacc.Bacc("TRN2", target_bir_lowering=False, num_devices=1)
    args = [nc.dram_tensor(n, a.shape, _mybir.dt.from_np(a.dtype), kind="ExternalInput").ap()
            for n, a in arrays.items()]
    args.append(nc.dram_tensor("out", x.shape, _mybir.dt.from_np(arrays["x"].dtype), kind="ExternalOutput").ap())
    gnn_resnorm(nc, *args)
    return _run(nc, [arrays], core_ids=[0]).results[0]["out"]
```
